# Optimizing a Trainium2 kernel written in Bass

```python
import numpy as np
import jax
import jax.numpy as jnp

def _softmax(x, axis=-1):
    return jax.nn.softmax(x, axis=axis)

def _gelu(x):
    return jax.nn.gelu(x, approximate=True)

def _silu(x):
    return jax.nn.silu(x)

def _sigmoid(x):
    return jax.nn.sigmoid(x)

def _layernorm(x, axis=-1, eps=1e-05):
    m = jnp.mean(x, axis=axis, keepdims=True)
    v = jnp.var(x, axis=axis, keepdims=True)
    return (x - m) / jnp.sqrt(v + eps)

def _scatter_add(tgt, idx, src, axis=0):
    return tgt.at[idx].add(src)

def _segment_sum(src, seg, n):
    return jax.ops.segment_sum(src, seg, n)
kernel_name = 'mk_adj_preln_d1_adj_r2_6e2dcc'

def setup_inputs(seed: int=0):
    np.random.seed(seed)
    _w = jnp.asarray

    def _rec_inputs():
        import jax
        import jax.numpy as jnp
        _gk = jax.random.key(seed)
        x = 7.22e-05 + 1 * jax.random.normal(jax.random.fold_in(_gk, 1), (64, 128, 256), jnp.float32)
        _a = jax.random.bernoulli(jax.random.fold_in(_gk, 2), 0.015625, (128, 128))
        _a = jnp.logical_or(_a, jnp.swapaxes(_a, -1, -2))
        _a = jnp.logical_or(_a, jnp.eye(128, dtype=bool))
        adj = _a.astype(jnp.int32)
        return (x, adj)
    x, adj = _rec_inputs()

    def _L0_gnn_setup():
        import jax, jax.numpy as jnp
        import numpy as np
        LEAKY_ALPHA = 0.01
        NEG_INF = -1000000000.0
        LN_EPS = 1e-05

        def _gat_heads(x, adj, W, a):
            O = W.shape[-1]
            Wh = jnp.einsum('bnf,hfo->bhno', x, W)
            f1 = jnp.einsum('bhno,ho->bhn', Wh, a[:, :O])
            f2 = jnp.einsum('bhno,ho->bhn', Wh, a[:, O:])
            e = f1[:, :, :, None] + f2[:, :, None, :]
            e = jnp.where(e > 0, e, LEAKY_ALPHA * e)
            e = jnp.where(adj[None, None] > 0, e, NEG_INF)
            attn = jax.nn.softmax(e, axis=-1)
            return jnp.einsum('bhnm,bhmo->bhno', attn, Wh)
        key = jax.random.key(seed)
        ks = jax.random.split(key, 10)
        B, N, F_in, F_hid, H, F_out, D_ff = (8, 1024, 256, 256, 4, 256, 256)
        s = 0.05
        return {'enc_inputs': jax.random.normal(ks[0], (B, N, F_in), jnp.float32), 'adj': jax.random.randint(ks[1], (N, N), 0, 2, jnp.int32), 'W_heads': jax.random.normal(ks[2], (H, F_in, F_hid), jnp.float32) * s, 'a_heads': jax.random.normal(ks[3], (H, 2 * F_hid), jnp.float32) * s, 'W_out': jax.random.normal(ks[4], (H * F_hid, F_out), jnp.float32) * s, 'a_out': jax.random.normal(ks[5], (2 * F_out,), jnp.float32) * s, 'w1': jax.random.normal(ks[6], (F_out, D_ff), jnp.float32) * s, 'b1': jnp.zeros((D_ff,), jnp.float32), 'w2': jax.random.normal(ks[7], (D_ff, F_out), jnp.float32) * s, 'b2': jnp.zeros((F_out,), jnp.float32), 'ln_gamma': jnp.ones((F_out,), jnp.float32), 'ln_beta': jnp.zeros((F_out,), jnp.float32)}
    _L0_gnn_all = _L0_gnn_setup()
    _L0_gnn_in = {k: v for k, v in _L0_gnn_all.items() if k in ('W_heads', 'a_heads', 'W_out', 'a_out', 'w1', 'b1', 'w2', 'b2', 'ln_gamma', 'ln_beta')}
    del _L0_gnn_all
    return {'x': x, 'adj': adj, 'L0_gnn_W_heads': _L0_gnn_in['W_heads'], 'L0_gnn_a_heads': _L0_gnn_in['a_heads'], 'L0_gnn_W_out': _L0_gnn_in['W_out'], 'L0_gnn_a_out': _L0_gnn_in['a_out'], 'L0_gnn_w1': _L0_gnn_in['w1'], 'L0_gnn_b1': _L0_gnn_in['b1'], 'L0_gnn_w2': _L0_gnn_in['w2'], 'L0_gnn_b2': _L0_gnn_in['b2'], 'L0_gnn_ln_gamma': _L0_gnn_in['ln_gamma'], 'L0_gnn_ln_beta': _L0_gnn_in['ln_beta']}

def reference(x, adj, L0_gnn_W_heads, L0_gnn_a_heads, L0_gnn_W_out, L0_gnn_a_out, L0_gnn_w1, L0_gnn_b1, L0_gnn_w2, L0_gnn_b2, L0_gnn_ln_gamma, L0_gnn_ln_beta):
    import jax
    import jax.numpy as jnp

    def _L0_gnn_ref(enc_inputs, adj, W_heads, a_heads, W_out, a_out, w1, b1, w2, b2, ln_gamma, ln_beta):
        import jax, jax.numpy as jnp
        import numpy as np
        LEAKY_ALPHA = 0.01
        NEG_INF = -1000000000.0
        LN_EPS = 1e-05

        def _gat_heads(x, adj, W, a):
            O = W.shape[-1]
            Wh = jnp.einsum('bnf,hfo->bhno', x, W)
            f1 = jnp.einsum('bhno,ho->bhn', Wh, a[:, :O])
            f2 = jnp.einsum('bhno,ho->bhn', Wh, a[:, O:])
            e = f1[:, :, :, None] + f2[:, :, None, :]
            e = jnp.where(e > 0, e, LEAKY_ALPHA * e)
            e = jnp.where(adj[None, None] > 0, e, NEG_INF)
            attn = jax.nn.softmax(e, axis=-1)
            return jnp.einsum('bhnm,bhmo->bhno', attn, Wh)
        B, N, _ = enc_inputs.shape
        h = jax.nn.elu(_gat_heads(enc_inputs, adj, W_heads, a_heads))
        h = jnp.transpose(h, (0, 2, 1, 3)).reshape(B, N, -1)
        out = _gat_heads(h, adj, W_out[None], a_out[None])[:, 0]
        out = jax.nn.elu(out)
        ffn = jnp.maximum(out @ w1 + b1, 0.0) @ w2 + b2
        y = ffn + out
        mu = jnp.mean(y, axis=-1, keepdims=True)
        var = jnp.var(y, axis=-1, keepdims=True)
        return (y - mu) / jnp.sqrt(var + LN_EPS) * ln_gamma + ln_beta
    h = jnp.maximum(_layernorm(x, axis=-1), 0.0)
    x = x + _L0_gnn_ref(h, adj, L0_gnn_W_heads, L0_gnn_a_heads, L0_gnn_W_out, L0_gnn_a_out, L0_gnn_w1, L0_gnn_b1, L0_gnn_w2, L0_gnn_b2, L0_gnn_ln_gamma, L0_gnn_ln_beta)
    return x

_drawn_inputs = setup_inputs


def setup_inputs(seed=0):
    import zlib

    import numpy as np

    out = dict(_drawn_inputs(seed))
    spreads = {'L0_gnn_b1': (0.0, 0.1),
     'L0_gnn_b2': (0.0, 0.1),
     'L0_gnn_ln_gamma': (1.0, 0.2),
     'L0_gnn_ln_beta': (0.0, 0.1)}
    factors = {}
    for name, (base, spread) in spreads.items():
        noise = np.random.default_rng([zlib.crc32(name.encode()), seed]).standard_normal(out[name].shape)
        drawn = base * np.exp(spread * noise) if base else spread * noise
        out[name] = jnp.asarray(drawn.astype(out[name].dtype))
    for name, factor in factors.items():
        out[name] = (out[name] * factor).astype(out[name].dtype)
    return out
```

```python
from contextlib import ExitStack

import numpy as np

import concourse.bass as bass
from concourse import mybir
from concourse.alu_op_type import AluOpType as ALU

F32 = mybir.dt.float32
F32R = mybir.dt.float32r
BF16 = mybir.dt.bfloat16
I32 = mybir.dt.int32
ACT = mybir.ActivationFunctionType
AX_X = mybir.AxisListType.X

P = 128
GB = 4
GN = GB * P
LEAKY = 0.01
LN_EPS = 1e-5
MASKED = 2.0 ** 127
PART = 32

PE_ORDER = """
    hT0@6 hT1@4 W1@7 W2@3 F@2 W3@0 P2@1 S0@2 S1@7 O0@1 O1@5 S2@6 W4@3 S3@2 W5@0 W6@7 M0@1 M1@6 PT0@4 W7@3
    PT1@5 Y0@6 Y1@2 Y2@1 G0@6 G1@0 Y3@7 G2@1 G3@2 PT2@4 N0@3 N1@6 PT3@7 G4@0 N2@5 N3@3 G5@4 G6@6 fT@7 G7@1
    R@2 W0@5
""".split()
ACT_ORDER = """
    Gh3 PTh3 Gh4 Nh1 Nh2 Nh3 Gh5 Gh6 fTh Gh7 LNr Ru Wn0 hTh0 hTh1 We0 Wn1 Re We1 Wn2 Wh0 Fh Wh1 We2 P2h Wn3
    Su0 We3 Su1 On0 Oe0 On1 Oe1 Oh0 Su2 Oh1 Se0 Su3 Wn4 Wh2 Wn5 We4 Se1 Mr0 Mh0 Mr1 Mh1 Se2 PTh0 Wh3 We5 Wn6
    Wh4 We6 PTh1 Wn7 Wh5 We7 Gh0 Wh6 Gh1 Wh7 Se3 Gh2 Nh0 PTh2 Yn
""".split()
DVE_ORDER = """
    LNs Nl3 Gl5 LNb fTl Gl6 Gl7 Rl Rm hTl0 hTl1 Wv0 Rr Wv1 Hh Fl Wv2 P2l Sl0 Sm0 Sl1 Ov0 Wv3 Ov1 Sm1 Sl2 Sm2
    Sr0 Wv4 Sr1 Ml0 Sl3 Ml1 Sm3 Sr2 Wv5 PTl0 Yb0 Wv6 PTl1 Yb1 Yb2 Wv7 Yb3 Yst Gl0 Sr3 Gl1 Ynb PTl2 Nl0 Gl2
    Gl3 PTl3 Nl1 Gl4 Yo Nl2
""".split()
POOL_ORDER = """
    LNp Rs Rp Wl0 Wl1 Hl Ss0 Ol0 Ol1 Ss1 Sp0 Ss2 Sp1 Wl2 Wl3 Sp2 Wl4 Wl5 Ss3 Wl6 Wl7 Yp Sp3 xb Yg
""".split()
AHEAD = """
    hT0 hT1 F S0 S1 S2 S3 PT0 PT1 G0 G1 G2 G3 PT2 PT3 G4 G5 G6 G7 W0 LNr hTh0 hTh1 Fh Su0 Su1 Su2 Se0 Su3
    Se1 Se2 PTh0 PTh1 Gh0 Gh1 Se3 Gh2 PTh2 LNs LNb hTl0 hTl1 Hh Fl Sl0 Sm0 Sl1 Sm1 Sl2 Sm2 Sr0 Sr1 Sl3 Sm3
    Sr2 PTl0 PTl1 Gl0 Sr3 Gl1 PTl2 Gl2 Gl3 PTl3 Gl4 LNp Hl Ss0 Ss1 Sp0 Ss2 Sp1 Sp2 Ss3 Sp3
""".split()
BEHIND = """
    P2 O0 O1 M0 M1 Y0 Y1 Y2 Y3 Nh1 Nh2 Nh3 fTh Ru Re P2h On0 Oe0 On1 Oe1 Oh0 Oh1 Mr0 Mh0 Mr1 Mh1 Yn Nl3 fTl
    Rl Rm Rr P2l Ov0 Ov1 Ml0 Ml1 Yb0 Yb1 Yb2 Yb3 Yst Ynb Yo Rs Rp Ol0 Ol1 Yp xb Yg
""".split()
BANK = {op.split("@")[0]: int(op.split("@")[1]) for op in PE_ORDER}
PE_ORDER = [op.split("@")[0] for op in PE_ORDER]


def part_of(op):
    return "ahead" if op in AHEAD else "behind" if op in BEHIND else "main"


def group_of(op, i):
    return i + {"ahead": 1, "main": 0, "behind": -1}[part_of(op)]


def split_name(op):
    if op in ("P2", "P2h", "P2l"):
        return op, 0
    return (op[:-1], int(op[-1])) if op[-1].isdigit() else (op, 0)


def gat_kernel(nc: bass.Bass, x, adj, W_heads, a_heads, W_out, a_out, w1, b1, w2, b2, ln_gamma, ln_beta, out):
    B, N, F = x.shape
    H = W_heads.shape[0]
    O1 = W_heads.shape[2]
    O2 = W_out.shape[1]
    D = w1.shape[1]
    NG = B // GB
    KF = F // P
    KH = H * O1 // P
    KO = O2 // P
    KD = D // P
    NAUG = O2 + 2
    assert N == P and H == GB and F == O1 == O2 == D == 256 and B % GB == 0 and NG >= 4

    x_g = x.rearrange("(g b) n f -> g n b f", b=GB)
    out_g = out.rearrange("(g b) n f -> g n b f", b=GB)

    with ExitStack() as ctx:
        def sb(name, shape, dt=F32):
            return ctx.enter_context(nc.sbuf_tensor(name, shape, dt))

        def sem(name):
            return ctx.enter_context(nc.semaphore(name))

        bank = [ctx.enter_context(nc.psum_tensor(f"bank{i}", [P, GN], F32)) for i in range(8)]

        def bank_of(kind, j=None):
            return bank[BANK[kind if j is None else f"{kind}{j}"]]

        ident = sb("ident", [P, P])
        ident_r = sb("ident_r", [P, P], F32R)
        ident_b = sb("ident_b", [P, P], BF16)
        mask = sb("mask", [P, GB, P], BF16)
        pick_f1 = sb("pick_f1", [P, GB, P], F32R)
        pick_f2 = sb("pick_f2", [P, GB, P], F32R)
        half_power = sb("half_power", [P, GB])
        wa_f = sb("wa_f", [P, KF, P])
        wa_h, wa_l = (sb(f"wa_{t}", [P, KF, P], F32R) for t in "hl")
        wh_h, wh_l = (sb(f"wheads_{t}", [P, H * KF, O1], F32R) for t in "hl")
        wo_a = sb("wo_a", [P, KH, 2])
        wo_h, wo_l = (sb(f"wout_{t}", [P, KH, NAUG], F32R) for t in "hl")
        w1_h, w1_l = (sb(f"w1_{t}", [P, KO, D], F32R) for t in "hl")
        w2_h, w2_l = (sb(f"w2_{t}", [P, KD, O2], F32R) for t in "hl")
        b1_col = sb("b1_col", [P, KD])
        b2_bc, gamma_bc, beta_bc = (sb(f"{t}_bc", [P, O2]) for t in ("b2", "gamma", "beta"))

        scratch = sb("scratch", [P, 12, GN])
        elu_out = [scratch[:, k, :] for k in range(4)]
        elu_exp = [scratch[:, 4 + k, :] for k in range(2)]
        o_exp = [scratch[:, 6 + k, :] for k in range(2)]
        o_f = [scratch[:, 8 + k, :] for k in range(2)]
        m_f = [scratch[:, 10 + k, :] for k in range(2)]
        x_in = sb("x_in", [P, GB, F])
        x_res = sb("x_res", [P, GB, F])
        y = sb("y", [P, GB, O2])
        h_f = sb("h_f", [P, GB, F])
        h_h, h_l = (sb(f"h_{t}", [P, GB, F], F32R) for t in "hl")
        blk_h, blk_l = (sb(f"blk_{t}", [P, 2, GN], F32R) for t in "hl")
        rows = sb("rows", [P, GN], F32R)
        rows2 = sb("rows2", [P, P], F32R)
        f2n = sb("f2n", [P, P])
        slope = [sb(f"slope{k}", [P, GB, P]) for k in range(3)]
        z = sb("z", [P, GB + 1, GB, P])
        zmax = sb("zmax", [P, GB + 1, GB])
        zsum = sb("zsum", [P, GB + 1, GB])
        zinv = sb("zinv", [P, GB + 1, GB])
        pt_h, pt_l = (sb(f"pt_{t}", [P, 2, GN], F32R) for t in "hl")
        p2_h, p2_l = (sb(f"p2_{t}", [P, GB, P], F32R) for t in "hl")
        g_h, g_l = (sb(f"g_{t}", [P, KF, H, GB, P], F32R) for t in "hl")
        h1_h, h1_l = (sb(f"h1_{t}", [P, KH, GN], F32R) for t in "hl")
        wh2_h, wh2_l = (sb(f"wh2_{t}", [P, GB, O2], F32R) for t in "hl")
        o_h, o_l = (sb(f"o_{t}", [P, KO, GN], F32R) for t in "hl")
        st1, st2 = (sb(f"st{k}", [P, GB, 6]) for k in (1, 2))
        mean1, mean2 = (sb(f"mean{k}", [P, GB]) for k in (1, 2))
        diff1, diff2 = (sb(f"diff{k}", [P, GB]) for k in (1, 2))
        ve1, ve2 = (sb(f"ve{k}", [P, GB]) for k in (1, 2))
        rstd1, rstd2 = (sb(f"rstd{k}", [P, GB]) for k in (1, 2))
        nbias1, nbias2 = (sb(f"nbias{k}", [P, GB]) for k in (1, 2))

        wheads_f = scratch[:, 0:4, :].rearrange("p a c -> p (a c)").rearrange("p (k o) -> p k o", o=O1)
        ffn_f = scratch[:, 4:6, :].rearrange("p a c -> p (a c)").rearrange("p (k o) -> p k o", o=O2)
        aout_f = scratch[:, 6, :]
        junk = [scratch[:, 7, k * O1:(k + 1) * O1] for k in range(2)]
        avec_f = [y, x_res]
        wout_f = [y, x_res]
        pick_f = [slope[0], slope[1]]

        x_in_ready, x_res_ready, out_stored = sem("x_in_ready"), sem("x_res_ready"), sem("out_stored")
        wheads_loaded, avec_loaded, wout_loaded, ffn_loaded = (sem(f"{t}_loaded") for t in ("wheads", "avec", "wout", "ffn"))
        aout_loaded, adj_loaded, vec_loaded = (sem(f"{t}_loaded") for t in ("aout", "adj", "vec"))
        patterns, consts, wa_steps, wa_ready, mask_ready, woa_ready = (
            sem(t) for t in ("patterns", "consts", "wa_steps", "wa_ready", "mask_ready", "woa_ready"))
        selected = sem("selected")
        wheads_high, wheads_low, late_high, late_low = (sem(t) for t in ("wheads_high", "wheads_low", "late_high", "late_low"))
        ln_stats, ln_step, ln_var, ln_rstd, ln_bias, ln_relu = (
            sem(f"ln_{t}") for t in ("stats", "step", "var", "rstd", "bias", "relu"))
        h_high, h_low, ht_mm, ht_high, ht_low, f_mm, f_high, f_low = (
            sem(t) for t in ("h_high", "h_low", "ht_mm", "ht_high", "ht_low", "f_mm", "f_high", "f_low"))
        s_mm, s_slope, s_leaky, s_max, s_shift, s_exp, s_sum, s_inv, s_prob = (
            sem(f"s_{t}") for t in ("mm", "slope", "leaky", "max", "shift", "exp", "sum", "inv", "prob"))
        pt_mm, pt_high, pt_low, g_mm, g_high, g_low = (
            sem(t) for t in ("pt_mm", "pt_high", "pt_low", "g_mm", "g_high", "g_low"))
        w_mm, w_neg, w_exp, w_elu, w_high, w_low = (sem(f"w_{t}") for t in ("mm", "neg", "exp", "elu", "high", "low"))
        n_mm, n_high, n_part, n_low = (sem(f"n_{t}") for t in ("mm", "high", "part", "low"))
        ft_mm, ft_high, ft_low = (sem(f"ft_{t}") for t in ("mm", "high", "low"))
        r_mm, r_slope, r_leaky, r_max, r_shift, r_exp, r_sum, r_inv, r_prob = (
            sem(f"r_{t}") for t in ("mm", "slope", "leaky", "max", "shift", "exp", "sum", "inv", "prob"))
        p2_mm, p2_high, p2_low = (sem(f"p2_{t}") for t in ("mm", "high", "low"))
        o_mm, o_neg, o_exp_done, o_elu, o_high, o_low = (sem(f"o_{t}") for t in ("mm", "neg", "exp_done", "elu", "high", "low"))
        m_mm, m_relu, m_high, m_low = (sem(f"m_{t}") for t in ("mm", "relu", "high", "low"))
        y_mm, y_bias, y_stats, y_step, y_var, y_rstd, y_nbias, y_norm, y_gamma, y_done, xb_ready = (
            sem(t) for t in ("y_mm", "y_bias", "y_stats", "y_step", "y_var", "y_rstd", "y_nbias", "y_norm", "y_gamma", "y_done", "xb_ready"))

        def wait(eng, s, n):
            if isinstance(n, int) and n <= 0:
                return
            eng.wait_ge(s, n)

        def all_steps(eng, order, ops, late, before, enter=None):
            everything = ("ahead", "main", "behind")

            def i_is_first(i):
                return isinstance(i, int) and i == -1

            def step(i, parts, parts_before):
                if enter:
                    enter(i, parts, parts_before)
                for op in order:
                    if i_is_first(i) and op == before:
                        late()
                    if part_of(op) in parts:
                        kind, j = split_name(op)
                        ops[kind](group_of(op, i), j)

            step(-1, ("ahead",), ())
            if before is None:
                late()
            step(0, ("ahead", "main"), ("ahead",))
            step(1, everything, ("ahead", "main"))
            with eng.Fori(2, NG - 1) as i:
                step(i, everything, everything)
            step(NG - 1, ("main", "behind"), everything)
            step(NG, ("behind",), ("main", "behind"))

        block = ctx.enter_context(nc.Block())

        @block.sync
        def _(sp):
            sp.dma_start(x_in[:], x_g[0]).then_inc(x_in_ready, 16)
            sp.dma_start(wheads_f, W_heads.rearrange("h (k p) o -> p (h k) o", p=P)).then_inc(wheads_loaded, 16)
            for k in range(2):
                sp.dma_start(avec_f[k][:].rearrange("p (a c) f -> p a (c f)", a=2),
                             a_heads[2 * k:2 * k + 2, :].unsqueeze(0).to_broadcast([P, 2, 2 * O1])).then_inc(avec_loaded, 16)
            sp.dma_start(z[:, GB, 0, :].bitcast(I32), adj).then_inc(adj_loaded, 16)
            for k, w in enumerate((w1, w2)):
                sp.dma_start(ffn_f[:, 2 * k:2 * k + 2, :], w.rearrange("(k p) o -> p k o", p=P)).then_inc(ffn_loaded, 16)
            sp.dma_start(aout_f, a_out.unsqueeze(0).to_broadcast([P, 2 * O2])).then_inc(aout_loaded, 16)
            for dst, src in ((b2_bc, b2), (gamma_bc, ln_gamma), (beta_bc, ln_beta)):
                sp.dma_start(dst[:], src.unsqueeze(0).to_broadcast([P, O2])).then_inc(vec_loaded, 16)
            with nc.allow_non_contiguous_dma("b1 as a column for each block"):
                sp.dma_start(b1_col[:], b1.rearrange("(k p) -> p k", p=P)).then_inc(vec_loaded, 16)
            sp.wait_ge(wa_ready, 1)
            for k in range(2):
                sp.dma_start(wout_f[k][:], W_out[k * 4 * P:(k + 1) * 4 * P, :].rearrange("(k p) o -> p k o", p=P)).then_inc(wout_loaded, 16)
            for g in (1, 2):
                sp.wait_ge(ln_relu, GB * g)
                sp.dma_start(x_in[:], x_g[g]).then_inc(x_in_ready, 16)
            sp.wait_ge(woa_ready, 1)
            sp.wait_ge(late_low, 4)
            sp.dma_start(x_res[:], x_g[0]).then_inc(x_res_ready, 16)

            def residual(g):
                sp.wait_ge(y_done, g)
                sp.dma_start(x_res[:], x_g[g]).then_inc(x_res_ready, 16)
                sp.dma_start(out_g[g - 1], y[:]).then_inc(out_stored, 16)

            with sp.Fori(1, NG - 2) as g:
                sp.wait_ge(ln_relu, GB * g + 2 * GB)
                sp.dma_start(x_in[:], x_g[g + 2]).then_inc(x_in_ready, 16)
                residual(g)
            residual(NG - 2)
            residual(NG - 1)
            sp.wait_ge(y_done, NG)
            sp.dma_start(out_g[NG - 1], y[:]).then_inc(out_stored, 16)
            sp.wait_ge(out_stored, 16 * NG)

        @block.tensor
        def _(pe):
            READ = {"PT": (pt_low, 4), "G": (g_low, 8), "W": (w_elu, 8), "N": (n_low, 4), "hT": (ht_low, 2),
                    "F": (f_low, 1), "S": (s_leaky, 4), "fT": (ft_low, 1), "R": (r_leaky, 1), "P2": (p2_low, 1),
                    "O": (o_elu, 2), "M": (m_relu, 2), "Y": (y_bias, 4)}
            now = {}

            def enter(i, parts, before):
                now.update(i=i, parts=parts, before=before)

            def wait_bank(kind, j=None):
                i, mine = now["i"], kind if j is None else f"{kind}{j}"
                users = [op for op in PE_ORDER if BANK[op] == BANK[mine]]
                present = [op for op in users if part_of(op) in now["parts"]]
                at = present.index(mine)
                if at == 0:
                    present, i = [op for op in users if part_of(op) in now["before"]], i - 1
                if present:
                    last = present[at - 1]
                    n, k = split_name(last)
                    read, per_group = READ[n]
                    wait(pe, read, per_group * group_of(last, i) + k + 1)

            def three(psum, pairs):
                n = len(pairs)
                for k, (lh, ll, rh, rl) in enumerate(pairs):
                    pe.matmul(psum, lh, rh, start=(k == 0), stop=False)
                    pe.matmul(psum, lh, rl, start=False, stop=False)
                    last = pe.matmul(psum, ll, rh, start=False, stop=(k == n - 1))
                return last

            def transposed(g, j):
                wait(pe, ln_relu, GB * g + GB)
                wait_bank("hT", j)
                for b in range(GB):
                    mm = pe.transpose(bank_of("hT", j)[:, b * P:(b + 1) * P], h_f[:, b, j * P:(j + 1) * P], ident[:])
                mm.then_inc(ht_mm, 1)

            def score_rows(g, j):
                wait(pe, ht_low, 2 * g + 2)
                wait_bank("F")
                three(bank_of("F")[:], [(wa_h[:, k, :], wa_l[:, k, :], blk_h[:, k, :], blk_l[:, k, :])
                                            for k in range(KF)]).then_inc(f_mm, 1)

            def scores(psum, f1_rows, f2_rows):
                pe.matmul(psum[:], ident_b[:], mask[:].rearrange("p a m -> p (a m)"), start=True, stop=False,
                          skip_group_check=True)
                pe.matmul(psum[:], f1_rows, pick_f1[:].rearrange("p a m -> p (a m)"), start=False, stop=False,
                          skip_group_check=True)
                for k in range(GB):
                    mm = pe.matmul(psum[:, k * P:(k + 1) * P], pick_f2[:, k, :], f2_rows[k], start=False,
                                   stop=(k == GB - 1), skip_group_check=True)
                return mm

            def score_tile(g, j):
                wait(pe, f_low, g + 1)
                wait_bank("S", j)
                mine = rows[:, j * P:(j + 1) * P]
                scores(bank_of("S", j), mine, [mine] * H).then_inc(s_mm, 1)

            def prob_turn(g, j):
                wait(pe, s_prob, GB * g + j + 1)
                wait_bank("PT", j)
                for k in range(H):
                    mm = pe.transpose(bank_of("PT", j)[:, k * P:(k + 1) * P], z[:, j, k, :], ident[:])
                mm.then_inc(pt_mm, 1)

            def attend(g, j):
                b, k = divmod(j, KF)
                wait(pe, pt_low, GB * g + b + 1)
                wait(pe, h_low, g + 1)
                wait_bank("G", j)
                cols = slice(k * P, (k + 1) * P)
                three(bank_of("G", j)[:], [(h_h[:, b, cols], h_l[:, b, cols], pt_h[:, b % 2, :], pt_l[:, b % 2, :])]
                      ).then_inc(g_mm, 1)

            def project(g, j):
                head, ob = divmod(j, O1 // P)
                wait(pe, g_low, GB * KF * g + GB * KF)
                wait_bank("W", j)
                cols = slice(ob * P, (ob + 1) * P)
                three(bank_of("W", j)[:], [
                    (wh_h[:, head * KF + k, cols], wh_l[:, head * KF + k, cols],
                     g_h[:, k, head, :, :].rearrange("p b n -> p (b n)"), g_l[:, k, head, :, :].rearrange("p b n -> p (b n)"))
                    for k in range(KF)]).then_inc(w_mm, 1)

            def project2(g, j):
                wait_bank("N", j)
                psum = bank_of("N", j)[:, 0:NAUG]
                cols = slice(j * P, (j + 1) * P)
                for k in range(KH):
                    if j == 0:
                        wait(pe, w_low, KH * g + k + 1)
                    pe.matmul(psum, h1_h[:, k, cols], wo_h[:, k, :], start=(k == 0), stop=False)
                    pe.matmul(psum, h1_h[:, k, cols], wo_l[:, k, :], start=False, stop=False)
                    mm = pe.matmul(psum, h1_l[:, k, cols], wo_h[:, k, :], start=False, stop=(k == KH - 1))
                mm.then_inc(n_mm, 1)

            def score_rows2(g, j):
                wait(pe, n_low, GB * g + GB)
                wait_bank("fT")
                pe.transpose(bank_of("fT")[:, 0:P], f2n[:], ident[:]).then_inc(ft_mm, 1)

            def score_tile2(g, j):
                wait(pe, ft_low, g + 1)
                wait_bank("R")
                scores(bank_of("R"), rows2[:], [rows2[:]] * GB).then_inc(r_mm, 1)

            def prob_turn2(g, j):
                wait(pe, r_prob, g + 1)
                wait_bank("P2")
                for b in range(GB):
                    mm = pe.transpose(bank_of("P2")[:, b * P:(b + 1) * P], z[:, GB, b, :], ident[:])
                mm.then_inc(p2_mm, 1)

            def attend2(g, j):
                wait(pe, p2_low, g + 1)
                wait_bank("O", j)
                cols = slice(j * P, (j + 1) * P)
                for b in range(GB):
                    n = slice(b * P, (b + 1) * P)
                    mm = three(bank_of("O", j)[:, n], [(wh2_h[:, b, cols], wh2_l[:, b, cols], p2_h[:, b, :], p2_l[:, b, :])])
                mm.then_inc(o_mm, 1)

            def mlp_in(g, j):
                wait(pe, o_low, KO * g + KO)
                wait_bank("M", j)
                cols = slice(j * P, (j + 1) * P)
                three(bank_of("M", j)[:], [(w1_h[:, k, cols], w1_l[:, k, cols], o_h[:, k, :], o_l[:, k, :])
                                            for k in range(KO)]).then_inc(m_mm, 1)

            def mlp_out(g, j):
                wait(pe, m_low, KD * g + KD)
                wait_bank("Y", j)
                psum = bank_of("Y", j)
                n = slice(j * P, (j + 1) * P)
                for k in range(KD):
                    pe.matmul(psum[:, 0:O2], blk_h[:, k, n], w2_h[:, k, :], start=(k == 0), stop=False, skip_group_check=True)
                    pe.matmul(psum[:, 0:O2], blk_h[:, k, n], w2_l[:, k, :], start=False, stop=False, skip_group_check=True)
                    pe.matmul(psum[:, 0:O2], blk_l[:, k, n], w2_h[:, k, :], start=False, stop=False, skip_group_check=True)
                for k in range(KO):
                    for part in (o_h, o_l):
                        mm = pe.matmul(psum[:, k * P:(k + 1) * P], part[:, k, n], ident_r[:], start=False,
                                       stop=(k == KO - 1 and part is o_l), skip_group_check=True)
                mm.then_inc(y_mm, 1)

            pe.wait_ge(consts, 5)
            pe.wait_ge(wa_ready, 1)
            pe.wait_ge(mask_ready, 1)

            pe.wait_ge(wheads_low, 1)

            def weights():
                pe.wait_ge(woa_ready, 1)
                pe.wait_ge(late_low, 4)

            all_steps(pe, PE_ORDER, {
                "hT": transposed, "F": score_rows, "S": score_tile, "PT": prob_turn, "G": attend, "W": project,
                "N": project2, "fT": score_rows2, "R": score_tile2, "P2": prob_turn2, "O": attend2, "M": mlp_in,
                "Y": mlp_out}, weights, None, enter)

        @block.scalar
        def _(act):
            def high(dst, src, ready, n, done):
                wait(act, ready, n)
                act.activation(dst, src, ACT.Copy).then_inc(done, 1)

            def ln_relu_op(g, j):
                wait(act, ln_bias, g + 1)
                wait(act, ht_mm, KF * g)
                wait(act, h_low, g)
                for b in range(GB):
                    act.activation(h_f[:, b, :], x_in[:, b, :], ACT.Relu, bias=nbias1[:, b:b + 1],
                                   scale=rstd1[:, b:b + 1]).then_inc(ln_relu, 1)

            def ht(g, j):
                wait(act, f_mm, g)
                wait(act, y_mm, GB * (g - 2))
                high(blk_h[:, j, :], bank_of("hT", j)[:], ht_mm, KF * g + j + 1, ht_high)

            def f(g, j):
                wait(act, s_mm, GB * g)
                high(rows[:], bank_of("F")[:], f_mm, g + 1, f_high)

            def slope_of(psum, buf, ready, n, done):
                wait(act, ready, n)
                act.activation(buf[:].rearrange("p a m -> p (a m)"), psum[:], ACT.Copy, scale=LEAKY).then_inc(done, 1)

            def s(g, j):
                wait(act, s_leaky, GB * g + j - 1)
                slope_of(bank_of("S", j), slope[j % 2], s_mm, GB * g + j + 1, s_slope)

            def r(g, j):
                wait(act, r_leaky, g)
                slope_of(bank_of("R"), slope[2], r_mm, g + 1, r_slope)

            def exps(tile, ready, n, done):
                wait(act, ready, n)
                act.activation(z[:, tile, :, :], z[:, tile, :, :], ACT.Exp).then_inc(done, 1)

            def pt(g, j):
                wait(act, g_mm, GB * KF * g + KF * (j - 1))
                high(pt_h[:, j % 2, :], bank_of("PT", j)[:], pt_mm, GB * g + j + 1, pt_high)

            def gg(g, j):
                wait(act, w_mm, KH * g)
                b, k = divmod(j, KF)
                high(g_h[:, k, :, b, :], bank_of("G", j)[:].rearrange("p (h n) -> p h n", h=H), g_mm,
                     GB * KF * g + j + 1, g_high)

            def w_first(g, j):
                wait(act, w_mm, KH * g + j + 1)
                wait(act, w_elu, KH * g + j - 1)
                act.activation(elu_exp[j % 2], bank_of("W", j)[:], ACT.Relu, scale=-1.0).then_inc(w_neg, 1)

            def w_second(g, j):
                wait(act, w_neg, KH * g + j + 1)
                act.activation(elu_exp[j % 2], elu_exp[j % 2], ACT.Exp, scale=-1.0).then_inc(w_exp, 1)

            def w_split(g, j):
                wait(act, n_mm, GB * g)
                high(h1_h[:, j, :], elu_out[j % 4], w_elu, KH * g + j + 1, w_high)

            def nn(g, j):
                wait(act, o_mm, KO * g)
                high(wh2_h[:, j, :], bank_of("N", j)[:, 0:O2], n_mm, GB * g + j + 1, n_high)

            def ft(g, j):
                high(rows2[:], bank_of("fT")[:, 0:P], ft_mm, g + 1, ft_high)

            def p2(g, j):
                high(p2_h[:].rearrange("p b n -> p (b n)"), bank_of("P2")[:], p2_mm, g + 1, p2_high)

            def o_first(g, j):
                wait(act, o_mm, KO * g + j + 1)
                wait(act, o_elu, KO * g + j - 1)
                act.activation(o_exp[j], bank_of("O", j)[:], ACT.Relu, scale=-1.0).then_inc(o_neg, 1)

            def o_second(g, j):
                wait(act, o_neg, KO * g + j + 1)
                act.activation(o_exp[j], o_exp[j], ACT.Exp, scale=-1.0).then_inc(o_exp_done, 1)

            def o_split(g, j):
                high(o_h[:, j, :], o_f[j], o_elu, KO * g + j + 1, o_high)

            def m(g, j):
                wait(act, m_mm, KD * g + j + 1)
                wait(act, m_low, KD * g + j - 1)
                act.activation(m_f[j], bank_of("M", j)[:], ACT.Relu, bias=b1_col[:, j:j + 1]).then_inc(m_relu, 1)

            def m_split(g, j):
                wait(act, f_mm, min(g + 3, NG) if isinstance(g, int) else g + 3)
                high(blk_h[:, j, :], m_f[j], m_relu, KD * g + j + 1, m_high)

            def y_norm_op(g, j):
                wait(act, y_nbias, g + 1)
                for b in range(GB):
                    act.activation(y[:, b, :], y[:, b, :], ACT.Identity, bias=nbias2[:, b:b + 1],
                                   scale=rstd2[:, b:b + 1]).then_inc(y_norm, 1)

            act.wait_ge(wheads_loaded, 16)
            act.activation(wh_h[:], wheads_f, ACT.Copy).then_inc(wheads_high, 1)

            def late():
                act.wait_ge(ffn_loaded, 32)
                act.activation(w1_h[:], ffn_f[:, 0:2, :], ACT.Copy).then_inc(late_high, 1)
                act.activation(w2_h[:], ffn_f[:, 2:4, :], ACT.Copy).then_inc(late_high, 1)
                act.wait_ge(wout_loaded, 32)
                for k in range(2):
                    act.activation(wo_h[:, 4 * k:4 * k + 4, 0:O2], wout_f[k][:], ACT.Copy).then_inc(late_high, 1)
                act.wait_ge(wheads_low, 1)
                act.wait_ge(late_low, 4)
                act.wait_ge(woa_ready, 1)

            all_steps(act, ACT_ORDER, {
                "LNr": ln_relu_op, "hTh": ht, "Fh": f, "Su": s, "Ru": r, "PTh": pt, "Gh": gg, "Wn": w_first,
                "We": w_second, "Wh": w_split, "Nh": nn, "fTh": ft, "P2h": p2, "On": o_first, "Oe": o_second,
                "Oh": o_split, "Mr": m, "Mh": m_split, "Yn": y_norm_op,
                "Se": lambda g, j: exps(j, s_shift, GB * g + j + 1, s_exp),
                "Re": lambda g, j: exps(GB, r_shift, g + 1, r_exp)}, late, "PTh0")

        @block.vector
        def _(dve):
            def low(dst, psum, high, ready, n, done):
                wait(dve, ready, n)
                dve.tensor_tensor(dst, psum, high.bitcast(F32), ALU.subtract).then_inc(done, 1)

            def stats(src, st, mean, diff, ve, g, s_stats, s_step, s_var):
                for b in range(GB):
                    dve.bn_stats(st[:, b, :], src[:, b, :]).then_inc(s_stats, 1)
                wait(dve, s_stats, GB * g + GB)
                dve.tensor_tensor(diff[:], st[:, :, 1], st[:, :, 4], ALU.subtract).then_inc(s_step, 1)
                dve.tensor_tensor(mean[:], st[:, :, 1], st[:, :, 4], ALU.add).then_inc(s_step, 1)
                dve.scalar_tensor_tensor(ve[:], st[:, :, 2], F * LN_EPS, st[:, :, 5], ALU.add, ALU.add).then_inc(s_step, 1)
                wait(dve, s_step, 5 * g + 3)
                dve.scalar_tensor_tensor(diff[:], diff[:], 0.25, diff[:], ALU.mult, ALU.mult).then_inc(s_step, 1)
                dve.tensor_scalar(mean[:], mean[:], 0.5, None, ALU.mult).then_inc(s_step, 1)
                wait(dve, s_step, 5 * g + 5)
                dve.scalar_tensor_tensor(ve[:], ve[:], 1.0 / F, diff[:], ALU.mult, ALU.add).then_inc(s_var, 1)

            def ln_stats_op(g, j):
                wait(dve, x_in_ready, 16 * g + 16)
                wait(dve, ln_rstd, g)
                stats(x_in, st1, mean1, diff1, ve1, g, ln_stats, ln_step, ln_var)

            def ln_bias_op(g, j):
                wait(dve, ln_rstd, g + 1)
                wait(dve, ln_relu, GB * g)
                dve.scalar_tensor_tensor(nbias1[:], mean1[:], -1.0, rstd1[:], ALU.mult, ALU.mult).then_inc(ln_bias, 1)

            def ht(g, j):
                low(blk_l[:, j, :], bank_of("hT", j)[:], blk_h[:, j, :], ht_high, KF * g + j + 1, ht_low)

            def h_split(g, j):
                wait(dve, ln_relu, GB * g + GB)
                wait(dve, g_mm, GB * KF * g)
                wait(dve, h_low, g)
                dve.tensor_copy(h_h[:], h_f[:]).then_inc(h_high, 1)

            def f(g, j):
                lows = slice(PART, 2 * PART)
                low(rows[lows, :], bank_of("F")[lows, :], rows[lows, :], f_high, g + 1, f_low)

            def leaky(tile, psum, buf, ready, done, n):
                wait(dve, ready, n)
                dve.tensor_tensor(z[:, tile, :, :].rearrange("p a m -> p (a m)"), psum[:],
                                  buf[:].rearrange("p a m -> p (a m)"), ALU.max).then_inc(done, 1)

            def row_max(tile, ready, done, n):
                wait(dve, ready, n)
                dve.tensor_reduce(zmax[:, tile, :], z[:, tile, :, :], AX_X, ALU.max).then_inc(done, 1)

            def sums(tile, ready, s_s, s_i, n):
                wait(dve, ready, n)
                dve.tensor_reduce(zsum[:, tile, :], z[:, tile, :, :], AX_X, ALU.add).then_inc(s_s, 1)
                wait(dve, s_s, n)
                dve.reciprocal(zinv[:, tile, :], zsum[:, tile, :]).then_inc(s_i, 1)

            def s_leaky_op(g, j):
                wait(dve, pt_mm, GB * (g - 1) + j + 1)
                leaky(j, bank_of("S", j), slope[j % 2], s_slope, s_leaky, GB * g + j + 1)

            def r_leaky_op(g, j):
                wait(dve, p2_mm, g)
                leaky(GB, bank_of("R"), slope[2], r_slope, r_leaky, g + 1)

            def pt(g, j):
                low(pt_l[:, j % 2, :], bank_of("PT", j)[:], pt_h[:, j % 2, :], pt_high, GB * g + j + 1, pt_low)

            def gg(g, j):
                b, k = divmod(j, KF)
                low(g_l[:, k, :, b, :], bank_of("G", j)[:].rearrange("p (h n) -> p h n", h=H), g_h[:, k, :, b, :],
                    g_high, GB * KF * g + j + 1, g_low)

            def w(g, j):
                wait(dve, w_exp, KH * g + j + 1)
                wait(dve, w_low, KH * g + j - 3)
                dve.scalar_tensor_tensor(elu_out[j % 4], elu_exp[j % 2], -1.0, bank_of("W", j)[:], ALU.add, ALU.max
                                         ).then_inc(w_elu, 1)

            def nn(g, j):
                psum = bank_of("N", j)
                wait(dve, ft_mm, g)
                low(wh2_l[:, j, :], psum[:, 0:O2], wh2_h[:, j, :], n_high, GB * g + j + 1, n_part)
                cols = f2n[:, 0:2 * PART].rearrange("p (r c) -> p r c", r=2)[:, :, j:j + GB + 1:GB]
                dve.tensor_copy(cols, psum[:, O2:NAUG].unsqueeze(1).to_broadcast([P, 2, 2])).then_inc(n_low, 1)

            def ft(g, j):
                lows = slice(PART, 2 * PART)
                low(rows2[lows, :], bank_of("fT")[lows, 0:P], rows2[lows, :], ft_high, g + 1, ft_low)

            def p2(g, j):
                low(p2_l[:].rearrange("p b n -> p (b n)"), bank_of("P2")[:], p2_h[:].rearrange("p b n -> p (b n)"),
                    p2_high, g + 1, p2_low)

            def o(g, j):
                wait(dve, o_exp_done, KO * g + j + 1)
                wait(dve, o_low, KO * g + j - 1)
                dve.scalar_tensor_tensor(o_f[j], o_exp[j], -1.0, bank_of("O", j)[:], ALU.add, ALU.max).then_inc(o_elu, 1)

            def m(g, j):
                low(blk_l[:, j, :], m_f[j], blk_h[:, j, :], m_high, KD * g + j + 1, m_low)

            def yy(g, j):
                wait(dve, y_mm, GB * g + j + 1)
                wait(dve, out_stored, 16 * g)
                dve.tensor_tensor(y[:, j, :], bank_of("Y", j)[:, 0:O2], b2_bc[:], ALU.add).then_inc(y_bias, 1)

            def y_stats_op(g, j):
                wait(dve, y_bias, GB * g + GB)
                stats(y, st2, mean2, diff2, ve2, g, y_stats, y_step, y_var)

            def y_nbias_op(g, j):
                wait(dve, y_rstd, g + 1)
                dve.scalar_tensor_tensor(nbias2[:], mean2[:], -1.0, rstd2[:], ALU.mult, ALU.mult).then_inc(y_nbias, 1)

            def y_last(g, j):
                wait(dve, y_gamma, g + 1)
                wait(dve, xb_ready, g + 1)
                dve.tensor_tensor(y[:], y[:], x_res[:], ALU.add).then_inc(y_done, 1)

            dve.memset(wa_f[:], 0.0).then_inc(wa_steps, 1)
            dve.wait_ge(wheads_loaded, 16)
            dve.wait_ge(avec_loaded, 32)
            for h in range(H):
                for k in range(KF):
                    for half in range(2):
                        a = avec_f[h // 2][:, 2 * (h % 2) + half, :]
                        dve.wait_ge(wa_steps, max(1, 2 * (h * KF + k) + half))
                        dve.tensor_tensor_reduce(junk[half], wheads_f[:, h * KF + k, :], a, 1.0, 0.0, ALU.mult, ALU.add,
                                                 wa_f[:, k, h + H * half:h + H * half + 1]).then_inc(wa_steps, 1)
            done = 1 + 2 * H * KF
            dve.wait_ge(wa_steps, done)
            dve.tensor_copy(wa_f[:, :, PART:PART + 2 * H], wa_f[:, :, 0:2 * H]).then_inc(wa_steps, 1)
            dve.wait_ge(wa_steps, done + 1)
            dve.tensor_copy(wa_h[:], wa_f[:]).then_inc(wa_steps, 1)
            dve.wait_ge(wa_steps, done + 2)
            dve.tensor_tensor(wa_l[:], wa_f[:], wa_h[:].bitcast(F32), ALU.subtract).then_inc(wa_ready, 1)
            dve.wait_ge(patterns, 7)
            dve.tensor_copy(ident_r[:], ident[:]).then_inc(consts, 1)
            dve.tensor_copy(ident_b[:], ident[:]).then_inc(consts, 1)
            dve.tensor_copy(pick_f1[:], pick_f[0][:]).then_inc(consts, 1)
            dve.tensor_copy(pick_f2[:], pick_f[1][:]).then_inc(consts, 1)
            dve.wait_ge(adj_loaded, 16)
            dve.tensor_scalar(z[:, GB, 1, :], z[:, GB, 0, :].bitcast(I32), 0, 1.0, ALU.is_gt, ALU.subtract).then_inc(consts, 1)
            dve.wait_ge(consts, 5)
            dve.tensor_scalar(mask[:], z[:, GB, 1, :].unsqueeze(1).to_broadcast([P, GB, P]), MASKED, None, ALU.mult
                              ).then_inc(mask_ready, 1)

            def late():
                dve.wait_ge(wout_loaded, 32)
                dve.wait_ge(aout_loaded, 16)
                dve.wait_ge(vec_loaded, 64)
                n = done + 2
                for k in range(KH):
                    for half in range(2):
                        dve.wait_ge(wa_steps, n + 2 * k + half - 1)
                        dve.tensor_tensor_reduce(junk[half], wout_f[k // 4][:, k % 4, :], aout_f[:, half * O2:(half + 1) * O2],
                                                 1.0, 0.0, ALU.mult, ALU.add, wo_a[:, k, half:half + 1]).then_inc(wa_steps, 1)
                n += 2 * KH
                dve.wait_ge(wa_steps, n)
                dve.tensor_copy(wo_h[:, :, O2:NAUG], wo_a[:]).then_inc(wa_steps, 1)
                dve.wait_ge(wa_steps, n + 1)
                dve.tensor_tensor(wo_l[:, :, O2:NAUG], wo_a[:], wo_h[:, :, O2:NAUG].bitcast(F32), ALU.subtract).then_inc(woa_ready, 1)

            all_steps(dve, DVE_ORDER, {
                "LNs": ln_stats_op, "LNb": ln_bias_op, "hTl": ht, "Hh": h_split, "Fl": f, "PTl": pt, "Gl": gg, "Wv": w,
                "Nl": nn, "fTl": ft, "P2l": p2, "Ov": o, "Ml": m, "Yb": yy, "Yst": y_stats_op, "Ynb": y_nbias_op,
                "Yo": y_last, "Sl": s_leaky_op, "Rl": r_leaky_op,
                "Sm": lambda g, j: row_max(j, s_leaky, s_max, GB * g + j + 1),
                "Rm": lambda g, j: row_max(GB, r_leaky, r_max, g + 1),
                "Sr": lambda g, j: sums(j, s_exp, s_sum, s_inv, GB * g + j + 1),
                "Rr": lambda g, j: sums(GB, r_exp, r_sum, r_inv, g + 1)}, late, "PTl0")

        @block.gpsimd
        def _(pool):
            def low(dst, value, high, ready, n, done):
                wait(pool, ready, n)
                pool.tensor_tensor(dst, value, high.bitcast(F32), ALU.subtract).then_inc(done, 1)

            def inverse_root(dst, var, ready, n, done):
                wait(pool, ready, n)
                pool.tensor_tensor(dst[:], var[:], half_power[:], ALU.pow).then_inc(done, 1)

            def ln_root(g, j):
                wait(pool, ln_relu, GB * g)
                inverse_root(rstd1, ve1, ln_var, g + 1, ln_rstd)

            def y_root(g, j):
                wait(pool, y_norm, GB * g)
                inverse_root(rstd2, ve2, y_var, g + 1, y_rstd)

            def h_split(g, j):
                low(h_l[:], h_f[:], h_h[:], h_high, g + 1, h_low)

            def by_block(tile, op, factors, ready, n, done):
                wait(pool, ready, n)
                pool.tensor_tensor(z[:, tile, :, :], z[:, tile, :, :],
                                   factors[:, tile, :].unsqueeze(2).to_broadcast([P, GB, P]), op).then_inc(done, 1)

            def w(g, j):
                low(h1_l[:, j, :], elu_out[j % 4], h1_h[:, j, :], w_high, KH * g + j + 1, w_low)

            def o(g, j):
                low(o_l[:, j, :], o_f[j], o_h[:, j, :], o_high, KO * g + j + 1, o_low)

            def residual(g, j):
                wait(pool, x_res_ready, 16 * g + 16)
                pool.tensor_tensor(x_res[:], x_res[:], beta_bc[:].unsqueeze(1).to_broadcast([P, GB, O2]), ALU.add
                                   ).then_inc(xb_ready, 1)

            def y_scale(g, j):
                wait(pool, y_norm, GB * g + GB)
                pool.tensor_tensor(y[:], y[:], gamma_bc[:].unsqueeze(1).to_broadcast([P, GB, O2]), ALU.mult
                                   ).then_inc(y_gamma, 1)

            pool.memset(half_power[:], -0.5).then_inc(patterns, 1)
            pool.memset(f2n[:], 0.0).then_inc(patterns, 1)
            pool.memset(ident[:], 0.0).then_inc(patterns, 1)
            pool.memset(pick_f[0][:], 0.0).then_inc(patterns, 1)
            pool.memset(pick_f[1][:], 0.0).then_inc(patterns, 1)
            pool.wait_ge(patterns, 5)
            pool.affine_select(out=ident[:], in_=ident[:], compare_op=ALU.not_equal, fill=1.0, base=0,
                               pattern=[[-1, P]], channel_multiplier=1).then_inc(patterns, 1)
            n_sel = 0
            for k in range(2):
                for part in range(2):
                    sel = pool.affine_select(out=pick_f[k][:], in_=pick_f[k][:], compare_op=ALU.not_equal, fill=1.0,
                                             base=-(H * k + PART * part), pattern=[[-1, GB], [0, P]], channel_multiplier=1)
                    n_sel += 1
                    if n_sel < 4:
                        sel.then_inc(selected, 1)
                        pool.wait_ge(selected, n_sel)
            sel.then_inc(patterns, 1)
            pool.wait_ge(wheads_high, 1)
            pool.tensor_tensor(wh_l[:], wheads_f, wh_h[:].bitcast(F32), ALU.subtract).then_inc(wheads_low, 1)

            def late():
                for k, (dst, src, hi) in enumerate((
                        (w1_l[:], ffn_f[:, 0:2, :], w1_h[:]), (w2_l[:], ffn_f[:, 2:4, :], w2_h[:]),
                        (wo_l[:, 0:4, 0:O2], wout_f[0][:], wo_h[:, 0:4, 0:O2]),
                        (wo_l[:, 4:8, 0:O2], wout_f[1][:], wo_h[:, 4:8, 0:O2]))):
                    pool.wait_ge(late_high, k + 1)
                    pool.tensor_tensor(dst, src, hi.bitcast(F32), ALU.subtract).then_inc(late_low, 1)
                pool.wait_ge(vec_loaded, 64)

            all_steps(pool, POOL_ORDER, {
                "LNp": ln_root, "Hl": h_split, "Wl": w, "Ol": o, "xb": residual, "Yp": y_root, "Yg": y_scale,
                "Ss": lambda g, j: by_block(j, ALU.subtract, zmax, s_max, GB * g + j + 1, s_shift),
                "Sp": lambda g, j: by_block(j, ALU.mult, zinv, s_inv, GB * g + j + 1, s_prob),
                "Rs": lambda g, j: by_block(GB, ALU.subtract, zmax, r_max, g + 1, r_shift),
                "Rp": lambda g, j: by_block(GB, ALU.mult, zinv, r_inv, g + 1, r_prob)}, late, "Ss3")


_INS = ["x", "adj", "L0_gnn_W_heads", "L0_gnn_a_heads", "L0_gnn_W_out", "L0_gnn_a_out", "L0_gnn_w1", "L0_gnn_b1",
        "L0_gnn_w2", "L0_gnn_b2", "L0_gnn_ln_gamma", "L0_gnn_ln_beta"]


def kernel(**inputs):
    import concourse.bacc as _bacc
    from concourse.bass_utils import run_bass_kernel_spmd as _run

    nc = _bacc.Bacc("TRN2", target_bir_lowering=False, num_devices=1, dynamic_dma_scratch_size=1024)
    arrays, args = {}, []
    for name in _INS:
        a = np.ascontiguousarray(inputs[name])
        arrays[f"in_{name}_dram"] = a
        args.append(nc.dram_tensor(f"in_{name}_dram", a.shape, mybir.dt.from_np(a.dtype), kind="ExternalInput").ap())
    shape = inputs["x"].shape
    out = nc.dram_tensor("out_dram", shape, F32, kind="ExternalOutput").ap()
    gat_kernel(nc, *args, out)
    r = _run(nc, [arrays], core_ids=[0])
    return r.results[0]["out_dram"]
```

```python
from contextlib import ExitStack

import numpy as np

import concourse.bass as bass
from concourse import mybir
from concourse.alu_op_type import AluOpType as ALU

F32 = mybir.dt.float32
F32R = mybir.dt.float32r
BF16 = mybir.dt.bfloat16
I32 = mybir.dt.int32
ACT = mybir.ActivationFunctionType
AX_X = mybir.AxisListType.X
AX_XY = mybir.AxisListType.XY

P = 128
GB = 4
GN = GB * P
LEAKY = 0.01
LN_EPS = 1e-5
MASKED = 2.0 ** 127
PART = 32

PE_ORDER = """
    W0@3 hT0@1 hT1@6 W1@0 W2@5 F@1 W3@3 P2@4 S0@7 S1@0 O0@5 O1@1 S2@6 W4@2 W5@0 oT0@5 oT1@6 S3@7 W6@1 PT0@5
    M0@3 M1@4 W7@2 PT1@4 G0@6 G1@7 Y0@5 G2@3 Y1@4 G3@1 N0@2 N1@0 PT2@5 PT3@4 N2@7 G4@3 N3@5 G5@6 G6@1 fT@0
    G7@7 R@2
""".split()
ACT_ORDER = """
    Gh7 LNr Ru Wn0 hTh0 hTh1 We0 Wn1 Re Wh0 Wn2 Fh We1 We2 P2h Wh1 Su0 Wn3 Su1 On0 On1 Oe0 Oe1 Su2 Wh2 Se0
    Wn4 We3 oTh0 oTh1 Se1 We4 Su3 Wn5 We5 Wh3 Mr0 PTh0 Mh0 Mr1 Mh1 Wn6 Wh4 PTh1 Wn7 We6 Wh5 We7 Wh6 Se2 Se3
    Wh7 Gh0 Gh1 Gh2 Nh0 Gh3 Yn PTh2 PTh3 Nh1 Gh4 Nh2 Nh3 Gh5 fTh Gh6
""".split()
DVE_ORDER = """
    LNs Nl2 Nl3 Gl4 Gl5 LNb fTl Gl6 Gl7 Rl Rm hTl0 hTl1 Wv0 Rr Hh Fl Wv1 Wv2 P2l Sl0 Sm0 Sl1 Sm1 Ov0 Ov1 Sl2
    Sr0 Wv3 oTl0 oTl1 Sr1 Wv4 Sm2 Wv5 Sl3 Sm3 PTl0 Ml0 Ml1 PTl1 Wv6 Yb0 Wv7 Yb1 Sr2 Yst Sr3 Ynb Gl0 Gl1 Gl2
    Gl3 Nl0 PTl2 PTl3 Nl1 Yo
""".split()
POOL_ORDER = """
    LNp xb Rs Rp Hl Wl0 Wl1 Ss0 Ss1 Wl2 Sp0 ob0 Sp1 Ss2 Wl3 ob1 Ss3 Wl4 Wl5 Wl6 Wl7 Sp2 Yp Sp3 Yg
""".split()
AHEAD = """
    hT0 hT1 F S0 S1 S2 S3 PT0 PT1 G0 G1 G2 G3 PT2 PT3 G4 G5 G6 G7 LNr hTh0 hTh1 Fh Su0 Su1 Su2 Se0 Se1 Su3
    PTh0 PTh1 Se2 Se3 Gh0 Gh1 Gh2 Gh3 PTh2 PTh3 Gh4 Gh5 Gh6 LNs LNb hTl0 hTl1 Hh Fl Sl0 Sm0 Sl1 Sm1 Sl2 Sr0
    Sr1 Sm2 Sl3 Sm3 PTl0 PTl1 Sr2 Sr3 Gl0 Gl1 Gl2 Gl3 PTl2 PTl3 LNp Hl Ss0 Ss1 Sp0 Sp1 Ss2 Ss3 Sp2 Sp3
""".split()
BEHIND = """
    P2 O0 O1 oT0 oT1 M0 M1 Y0 Y1 Ru Re P2h On0 On1 Oe0 Oe1 oTh0 oTh1 Mr0 Mh0 Mr1 Mh1 Yn Nl2 Nl3 fTl Rl Rm Rr
    P2l Ov0 Ov1 oTl0 oTl1 Ml0 Ml1 Yb0 Yb1 Yst Ynb Yo xb Rs Rp ob0 ob1 Yp Yg
""".split()
BANK = {op.split("@")[0]: int(op.split("@")[1]) for op in PE_ORDER}
PE_ORDER = [op.split("@")[0] for op in PE_ORDER]


def part_of(op):
    return "ahead" if op in AHEAD else "behind" if op in BEHIND else "main"


def group_of(op, i):
    return i + {"ahead": 1, "main": 0, "behind": -1}[part_of(op)]


def split_name(op):
    if op in ("P2", "P2h", "P2l"):
        return op, 0
    return (op[:-1], int(op[-1])) if op[-1].isdigit() else (op, 0)


def gat_kernel(nc: bass.Bass, x, adj, W_heads, a_heads, W_out, a_out, w1, b1, w2, b2, ln_gamma, ln_beta, out):
    B, N, F = x.shape
    H = W_heads.shape[0]
    O1 = W_heads.shape[2]
    O2 = W_out.shape[1]
    D = w1.shape[1]
    NG = B // GB
    KF = F // P
    KH = H * O1 // P
    KO = O2 // P
    KD = D // P
    NAUG = O2 + 2
    assert N == P and H == GB and F == O1 == O2 == D == 256 and B % GB == 0 and NG >= 4

    x_g = x.rearrange("(g b) n f -> g n b f", b=GB)
    out_g = out.rearrange("(g b) n f -> g n b f", b=GB)

    with ExitStack() as ctx:
        def sb(name, shape, dt=F32):
            return ctx.enter_context(nc.sbuf_tensor(name, shape, dt))

        def sem(name):
            return ctx.enter_context(nc.semaphore(name))

        bank = [ctx.enter_context(nc.psum_tensor(f"bank{i}", [P, GN], F32)) for i in range(8)]

        def bank_of(kind, j=None):
            return bank[BANK[kind if j is None else f"{kind}{j}"]]

        ident = sb("ident", [P, P])
        ident_b = sb("ident_b", [P, P], BF16)
        mask = sb("mask", [P, GB, P], BF16)
        pick_f1 = sb("pick_f1", [P, GB, P], F32R)
        pick_f2 = sb("pick_f2", [P, GB, P], F32R)
        picks = sb("picks", [P, 2 * H])
        half_power = sb("half_power", [P, GB])
        wa_f = sb("wa_f", [P, KF, P])
        wa_h = sb("wa_h", [P, KF, P], F32R)
        wa_hl = sb("wa_hl", [P, KF, P], F32R)
        wh_h, wh_l = (sb(f"wheads_{t}", [P, H * KF, O1], F32R) for t in "hl")
        wo_a = sb("wo_a", [P, KH, 2])
        wo_h, wo_l = (sb(f"wout_{t}", [P, KH, NAUG], F32R) for t in "hl")
        w1_h, w1_l = (sb(f"w1_{t}", [P, KO, D], F32R) for t in "hl")
        w2_h, w2_l = (sb(f"w2_{t}", [P, KD, O2], F32R) for t in "hl")
        b1_col = sb("b1_col", [P, KD])
        b2_bc, gamma_bc, beta_bc = (sb(f"{t}_bc", [P, O2]) for t in ("b2", "gamma", "beta"))

        scratch = sb("scratch", [P, 12, GN])
        elu_out = [scratch[:, k, :] for k in range(4)]
        elu_exp = [scratch[:, 4 + k, :] for k in range(2)]
        o_exp = [scratch[:, 6 + k, :] for k in range(2)]
        o_f = [scratch[:, 8 + k, :].rearrange("p (b c) -> p b c", b=2) for k in range(2)]
        m_f = [scratch[:, 10 + k, :] for k in range(2)]
        x_in = sb("x_in", [P, GB, F])
        x_res = sb("x_res", [P, GB, F])
        y = sb("y", [P, GB, O2])
        h_f = sb("h_f", [P, GB, F])
        h_h, h_l = (sb(f"h_{t}", [P, GB, F], F32R) for t in "hl")
        blk_h, blk_l = (sb(f"blk_{t}", [P, 2, GN], F32R) for t in "hl")
        rows = sb("rows", [P, GN], F32R)
        rows2 = sb("rows2", [P, P], F32R)
        f2n = sb("f2n", [P, P])
        slope = [sb(f"slope{k}", [P, GB, P]) for k in range(3)]
        z = sb("z", [P, GB + 1, GB, P])
        zmax = sb("zmax", [P, GB + 1, GB])
        zsum = sb("zsum", [P, GB + 1, GB])
        zinv = sb("zinv", [P, GB + 1, GB])
        pt_h, pt_l = (sb(f"pt_{t}", [P, 2, GN], F32R) for t in "hl")
        p2_h, p2_l = (sb(f"p2_{t}", [P, GB, P], F32R) for t in "hl")
        g_h, g_l = (sb(f"g_{t}", [P, KF, H, GB, P], F32R) for t in "hl")
        h1_h, h1_l = (sb(f"h1_{t}", [P, KH, GN], F32R) for t in "hl")
        wh2_h, wh2_l = (sb(f"wh2_{t}", [P, GB, O2], F32R) for t in "hl")
        o_h, o_l = (sb(f"o_{t}", [P, KO, GN], F32R) for t in "hl")
        st1, st2 = (sb(f"st{k}", [P, GB, 6]) for k in (1, 2))
        mean1, mean2 = (sb(f"mean{k}", [P, GB]) for k in (1, 2))
        diff1, diff2 = (sb(f"diff{k}", [P, GB]) for k in (1, 2))
        ve1, ve2 = (sb(f"ve{k}", [P, GB]) for k in (1, 2))
        rstd1, rstd2 = (sb(f"rstd{k}", [P, GB]) for k in (1, 2))
        nbias1, nbias2 = (sb(f"nbias{k}", [P, GB]) for k in (1, 2))

        wheads_f = scratch[:, 0:4, :].rearrange("p a c -> p (a c)").rearrange("p (k o) -> p k o", o=O1)
        ffn_f = scratch[:, 6:8, :].rearrange("p a c -> p (a c)").rearrange("p (k o) -> p k o", o=O2)
        wout_f = scratch[:, 8:12, :].rearrange("p a c -> p (a c)").rearrange("p (k o) -> p k o", o=O2)
        aout_f = slope[2][:].rearrange("p b n -> p (b n)")
        junk = [slope[0][:, 2 * k:2 * k + 2, :].rearrange("p b n -> p (b n)") for k in range(2)]
        junk2 = [y[:, k, :] for k in range(2)]
        avec_f = [y, x_res]

        x_in_ready, x_res_ready, out_stored = sem("x_in_ready"), sem("x_res_ready"), sem("out_stored")
        wheads_loaded, avec_loaded, wout_loaded, ffn_loaded = (sem(f"{t}_loaded") for t in ("wheads", "avec", "wout", "ffn"))
        aout_loaded, adj_loaded, vec_loaded = (sem(f"{t}_loaded") for t in ("aout", "adj", "vec"))
        patterns, consts, wa_steps, wa_ready, mask_ready, woa_ready = (
            sem(t) for t in ("patterns", "consts", "wa_steps", "wa_ready", "mask_ready", "woa_ready"))
        wheads_high, wheads_low, late_high, late_low = (sem(t) for t in ("wheads_high", "wheads_low", "late_high", "late_low"))
        ln_stats, ln_step, ln_var, ln_rstd, ln_bias, ln_relu = (
            sem(f"ln_{t}") for t in ("stats", "step", "var", "rstd", "bias", "relu"))
        h_high, h_low, ht_mm, ht_high, ht_low, f_mm, f_high, f_low = (
            sem(t) for t in ("h_high", "h_low", "ht_mm", "ht_high", "ht_low", "f_mm", "f_high", "f_low"))
        s_mm, s_slope, s_leaky, s_max, s_shift, s_exp, s_sum, s_inv, s_prob = (
            sem(f"s_{t}") for t in ("mm", "slope", "leaky", "max", "shift", "exp", "sum", "inv", "prob"))
        pt_mm, pt_high, pt_low, g_mm, g_high, g_low = (
            sem(t) for t in ("pt_mm", "pt_high", "pt_low", "g_mm", "g_high", "g_low"))
        w_mm, w_neg, w_exp, w_elu, w_high, w_low = (sem(f"w_{t}") for t in ("mm", "neg", "exp", "elu", "high", "low"))
        n_mm, n_high, n_part, n_low = (sem(f"n_{t}") for t in ("mm", "high", "part", "low"))
        ft_mm, ft_high, ft_low = (sem(f"ft_{t}") for t in ("mm", "high", "low"))
        r_mm, r_slope, r_leaky, r_max, r_shift, r_exp, r_sum, r_inv, r_prob = (
            sem(f"r_{t}") for t in ("mm", "slope", "leaky", "max", "shift", "exp", "sum", "inv", "prob"))
        p2_mm, p2_high, p2_low = (sem(f"p2_{t}") for t in ("mm", "high", "low"))
        o_mm, o_neg, o_exp_done, o_elu, o_bias = (sem(f"o_{t}") for t in ("mm", "neg", "exp_done", "elu", "bias"))
        ot_mm, ot_high, ot_low = (sem(f"ot_{t}") for t in ("mm", "high", "low"))
        m_mm, m_relu, m_high, m_low = (sem(f"m_{t}") for t in ("mm", "relu", "high", "low"))
        y_mm, y_sum, y_stats, y_step, y_var, y_rstd, y_nbias, y_norm, y_gamma, y_done, xb_ready = (
            sem(t) for t in ("y_mm", "y_sum", "y_stats", "y_step", "y_var", "y_rstd", "y_nbias", "y_norm", "y_gamma", "y_done", "xb_ready"))

        def wait(eng, s, n):
            if isinstance(n, int) and n <= 0:
                return
            eng.wait_ge(s, n)

        def all_steps(eng, order, ops, setup, enter=None):
            everything = ("ahead", "main", "behind")
            setup = dict(setup)

            def step(i, parts, parts_before):
                if enter:
                    enter(i, parts, parts_before)
                for op in order:
                    if part_of(op) in parts:
                        if isinstance(i, int) and (i, op) in setup:
                            setup.pop((i, op))()
                        kind, j = split_name(op)
                        ops[kind](group_of(op, i), j)

            step(-1, ("ahead",), ())
            step(0, ("ahead", "main"), ("ahead",))
            step(1, everything, ("ahead", "main"))
            with eng.Fori(2, NG - 1) as i:
                step(i, everything, everything)
            step(NG - 1, ("main", "behind"), everything)
            step(NG, ("behind",), ("main", "behind"))
            assert not setup

        block = ctx.enter_context(nc.Block())

        @block.sync
        def _(sp):
            sp.dma_start(x_in[:], x_g[0]).then_inc(x_in_ready, 16)
            sp.dma_start(wheads_f, W_heads.rearrange("h (k p) o -> p (h k) o", p=P)).then_inc(wheads_loaded, 16)
            for k in range(2):
                sp.dma_start(avec_f[k][:].rearrange("p (a c) f -> p a (c f)", a=2),
                             a_heads[2 * k:2 * k + 2, :].unsqueeze(0).to_broadcast([P, 2, 2 * O1])).then_inc(avec_loaded, 16)
            sp.dma_start(z[:, GB, 0, :].bitcast(I32), adj).then_inc(adj_loaded, 16)
            sp.dma_start(wout_f, W_out.rearrange("(k p) o -> p k o", p=P)).then_inc(wout_loaded, 16)
            for k, w in enumerate((w1, w2)):
                sp.dma_start(ffn_f[:, 2 * k:2 * k + 2, :], w.rearrange("(k p) o -> p k o", p=P)).then_inc(ffn_loaded, 16)
            sp.dma_start(aout_f, a_out.unsqueeze(0).to_broadcast([P, 2 * O2])).then_inc(aout_loaded, 16)
            for dst, src in ((b2_bc, b2), (gamma_bc, ln_gamma), (beta_bc, ln_beta)):
                sp.dma_start(dst[:], src.unsqueeze(0).to_broadcast([P, O2])).then_inc(vec_loaded, 16)
            with nc.allow_non_contiguous_dma("b1 as a column for each block"):
                sp.dma_start(b1_col[:], b1.rearrange("(k p) -> p k", p=P)).then_inc(vec_loaded, 16)
            for g in (1, 2):
                sp.wait_ge(ln_relu, GB * g)
                sp.dma_start(x_in[:], x_g[g]).then_inc(x_in_ready, 16)
                if g == 1:
                    sp.wait_ge(wa_ready, 2)
                    sp.dma_start(x_res[:], x_g[0]).then_inc(x_res_ready, 16)

            def residual(g):
                sp.wait_ge(y_done, g)
                sp.dma_start(x_res[:], x_g[g]).then_inc(x_res_ready, 16)
                sp.dma_start(out_g[g - 1], y[:]).then_inc(out_stored, 16)

            with sp.Fori(1, NG - 2) as g:
                sp.wait_ge(ln_relu, GB * g + 2 * GB)
                sp.dma_start(x_in[:], x_g[g + 2]).then_inc(x_in_ready, 16)
                residual(g)
            residual(NG - 2)
            residual(NG - 1)
            sp.wait_ge(y_done, NG)
            sp.dma_start(out_g[NG - 1], y[:]).then_inc(out_stored, 16)
            sp.wait_ge(out_stored, 16 * NG)

        @block.tensor
        def _(pe):
            READ = {"PT": (pt_low, 4), "G": (g_low, 8), "W": (w_elu, 8), "N": (n_low, 4), "hT": (ht_low, 2),
                    "F": (f_low, 1), "S": (s_leaky, 4), "fT": (ft_low, 1), "R": (r_leaky, 1), "P2": (p2_low, 1),
                    "O": (o_elu, 2), "oT": (ot_low, 2), "M": (m_relu, 2), "Y": (y_sum, 2)}
            now = {}

            def enter(i, parts, before):
                now.update(i=i, parts=parts, before=before)

            def wait_bank(kind, j=None):
                i, mine = now["i"], kind if j is None else f"{kind}{j}"
                users = [op for op in PE_ORDER if BANK[op] == BANK[mine]]
                present = [op for op in users if part_of(op) in now["parts"]]
                at = present.index(mine)
                if at == 0:
                    present, i = [op for op in users if part_of(op) in now["before"]], i - 1
                if present:
                    last = present[at - 1]
                    n, k = split_name(last)
                    read, per_group = READ[n]
                    wait(pe, read, per_group * group_of(last, i) + k + 1)

            def three(psum, pairs):
                n = len(pairs)
                for k, (lh, ll, rh, rl) in enumerate(pairs):
                    pe.matmul(psum, lh, rh, start=(k == 0), stop=False)
                    pe.matmul(psum, lh, rl, start=False, stop=False)
                    last = pe.matmul(psum, ll, rh, start=False, stop=(k == n - 1))
                return last

            def transposed(g, j):
                wait(pe, ln_relu, GB * g + GB)
                wait_bank("hT", j)
                for b in range(GB):
                    mm = pe.transpose(bank_of("hT", j)[:, b * P:(b + 1) * P], h_f[:, b, j * P:(j + 1) * P], ident[:])
                mm.then_inc(ht_mm, 1)

            def score_rows(g, j):
                wait(pe, ht_low, 2 * g + 2)
                wait_bank("F")
                for k in range(KF):
                    pe.matmul(bank_of("F")[:], wa_hl[:, k, :], blk_h[:, k, :], start=(k == 0), stop=False)
                    mm = pe.matmul(bank_of("F")[:], wa_h[:, k, :], blk_l[:, k, :], start=False, stop=(k == KF - 1))
                mm.then_inc(f_mm, 1)

            def scores(psum, f1_rows, f2_rows):
                pe.matmul(psum[:], ident_b[:], mask[:].rearrange("p a m -> p (a m)"), start=True, stop=False,
                          skip_group_check=True)
                pe.matmul(psum[:], f1_rows, pick_f1[:].rearrange("p a m -> p (a m)"), start=False, stop=False,
                          skip_group_check=True)
                for k in range(GB):
                    mm = pe.matmul(psum[:, k * P:(k + 1) * P], pick_f2[:, k, :], f2_rows[k], start=False,
                                   stop=(k == GB - 1), skip_group_check=True)
                return mm

            def score_tile(g, j):
                wait(pe, f_low, g + 1)
                wait_bank("S", j)
                mine = rows[:, j * P:(j + 1) * P]
                scores(bank_of("S", j), mine, [mine] * H).then_inc(s_mm, 1)

            def prob_turn(g, j):
                wait(pe, s_prob, GB * g + j + 1)
                wait_bank("PT", j)
                for k in range(H):
                    mm = pe.transpose(bank_of("PT", j)[:, k * P:(k + 1) * P], z[:, j, k, :], ident[:])
                mm.then_inc(pt_mm, 1)

            def attend(g, j):
                b, k = divmod(j, KF)
                wait(pe, pt_low, GB * g + b + 1)
                wait(pe, h_low, g + 1)
                wait_bank("G", j)
                cols = slice(k * P, (k + 1) * P)
                three(bank_of("G", j)[:], [(h_h[:, b, cols], h_l[:, b, cols], pt_h[:, b % 2, :], pt_l[:, b % 2, :])]
                      ).then_inc(g_mm, 1)

            def project(g, j):
                head, ob = divmod(j, O1 // P)
                wait(pe, g_low, GB * KF * g + GB * KF)
                wait_bank("W", j)
                cols = slice(ob * P, (ob + 1) * P)
                three(bank_of("W", j)[:], [
                    (wh_h[:, head * KF + k, cols], wh_l[:, head * KF + k, cols],
                     g_h[:, k, head, :, :].rearrange("p b n -> p (b n)"), g_l[:, k, head, :, :].rearrange("p b n -> p (b n)"))
                    for k in range(KF)]).then_inc(w_mm, 1)

            def project2(g, j):
                wait_bank("N", j)
                psum = bank_of("N", j)[:, 0:NAUG]
                cols = slice(j * P, (j + 1) * P)
                for k in range(KH):
                    if j == 0:
                        wait(pe, w_low, KH * g + k + 1)
                    pe.matmul(psum, h1_h[:, k, cols], wo_h[:, k, :], start=(k == 0), stop=False)
                    pe.matmul(psum, h1_h[:, k, cols], wo_l[:, k, :], start=False, stop=False)
                    mm = pe.matmul(psum, h1_l[:, k, cols], wo_h[:, k, :], start=False, stop=(k == KH - 1))
                mm.then_inc(n_mm, 1)

            def score_rows2(g, j):
                wait(pe, n_low, GB * g + GB)
                wait_bank("fT")
                pe.transpose(bank_of("fT")[:, 0:P], f2n[:], ident[:]).then_inc(ft_mm, 1)

            def score_tile2(g, j):
                wait(pe, ft_low, g + 1)
                wait_bank("R")
                scores(bank_of("R"), rows2[:], [rows2[:]] * GB).then_inc(r_mm, 1)

            def prob_turn2(g, j):
                wait(pe, r_prob, g + 1)
                wait_bank("P2")
                for b in range(GB):
                    mm = pe.transpose(bank_of("P2")[:, b * P:(b + 1) * P], z[:, GB, b, :], ident[:])
                mm.then_inc(p2_mm, 1)

            def attend2(g, j):
                wait(pe, p2_low, g + 1)
                wait_bank("O", j)
                for k in range(2):
                    b = 2 * j + k
                    mm = three(bank_of("O", j)[:, k * O2:(k + 1) * O2], [(p2_h[:, b, :], p2_l[:, b, :], wh2_h[:, b, :], wh2_l[:, b, :])])
                mm.then_inc(o_mm, 1)

            def turn_o(g, j):
                wait(pe, o_elu, 2 * g + 2)
                wait_bank("oT", j)
                for b in range(GB):
                    mm = pe.transpose(bank_of("oT", j)[:, b * P:(b + 1) * P], o_f[b // 2][:, b % 2, j * P:(j + 1) * P], ident[:])
                mm.then_inc(ot_mm, 1)

            def mlp_in(g, j):
                wait(pe, ot_low, KO * g + KO)
                wait_bank("M", j)
                cols = slice(j * P, (j + 1) * P)
                three(bank_of("M", j)[:], [(w1_h[:, k, cols], w1_l[:, k, cols], o_h[:, k, :], o_l[:, k, :])
                                            for k in range(KO)]).then_inc(m_mm, 1)

            def mlp_out(g, j):
                wait(pe, m_low, KD * g + KD)
                wait_bank("Y", j)
                for b in range(2):
                    n = slice((2 * j + b) * P, (2 * j + b + 1) * P)
                    mm = three(bank_of("Y", j)[:, b * O2:(b + 1) * O2],
                               [(blk_h[:, k, n], blk_l[:, k, n], w2_h[:, k, :], w2_l[:, k, :]) for k in range(KD)])
                mm.then_inc(y_mm, 1)

            def constants():
                pe.wait_ge(wa_ready, 2)
                pe.wait_ge(consts, 5)
                pe.wait_ge(mask_ready, 1)

            def wheads():
                pe.wait_ge(wheads_low, 1)

            def late_weights():
                pe.wait_ge(woa_ready, 1)
                pe.wait_ge(late_low, 3)

            pe.wait_ge(patterns, 4)
            all_steps(pe, PE_ORDER, {
                "hT": transposed, "F": score_rows, "S": score_tile, "PT": prob_turn, "G": attend, "W": project,
                "N": project2, "fT": score_rows2, "R": score_tile2, "P2": prob_turn2, "O": attend2, "oT": turn_o, "M": mlp_in,
                "Y": mlp_out},
                {(-1, "F"): constants, (-1 if part_of("W0") == "ahead" else 0, "W0"): wheads, (0, "N0"): late_weights}, enter)

        @block.scalar
        def _(act):
            def high(dst, src, ready, n, done):
                wait(act, ready, n)
                act.activation(dst, src, ACT.Copy).then_inc(done, 1)

            def ln_relu_op(g, j):
                wait(act, ln_bias, g + 1)
                wait(act, ht_mm, KF * g)
                wait(act, h_low, g)
                for b in range(GB):
                    act.activation(h_f[:, b, :], x_in[:, b, :], ACT.Relu, bias=nbias1[:, b:b + 1],
                                   scale=rstd1[:, b:b + 1]).then_inc(ln_relu, 1)

            def ht(g, j):
                wait(act, f_mm, g)
                wait(act, y_mm, 2 * (g - 2))
                high(blk_h[:, j, :], bank_of("hT", j)[:], ht_mm, KF * g + j + 1, ht_high)

            def f(g, j):
                wait(act, s_mm, GB * g)
                high(rows[:], bank_of("F")[:], f_mm, g + 1, f_high)

            def slope_of(psum, buf, ready, n, done):
                wait(act, ready, n)
                act.activation(buf[:].rearrange("p a m -> p (a m)"), psum[:], ACT.Copy, scale=LEAKY).then_inc(done, 1)

            def s(g, j):
                wait(act, s_leaky, GB * g + j - 1)
                slope_of(bank_of("S", j), slope[j % 2], s_mm, GB * g + j + 1, s_slope)

            def r(g, j):
                wait(act, r_leaky, g)
                slope_of(bank_of("R"), slope[2], r_mm, g + 1, r_slope)

            def exps(tile, ready, n, done):
                wait(act, ready, n)
                act.activation(z[:, tile, :, :], z[:, tile, :, :], ACT.Exp).then_inc(done, 1)

            def pt(g, j):
                wait(act, g_mm, GB * KF * g + KF * (j - 1))
                high(pt_h[:, j % 2, :], bank_of("PT", j)[:], pt_mm, GB * g + j + 1, pt_high)

            def gg(g, j):
                wait(act, w_mm, KH * g)
                b, k = divmod(j, KF)
                high(g_h[:, k, :, b, :], bank_of("G", j)[:].rearrange("p (h n) -> p h n", h=H), g_mm,
                     GB * KF * g + j + 1, g_high)

            def w_first(g, j):
                wait(act, w_mm, KH * g + j + 1)
                wait(act, w_elu, KH * g + j - 1)
                act.activation(elu_exp[j % 2], bank_of("W", j)[:], ACT.Relu, scale=-1.0).then_inc(w_neg, 1)

            def w_second(g, j):
                wait(act, w_neg, KH * g + j + 1)
                act.activation(elu_exp[j % 2], elu_exp[j % 2], ACT.Exp, scale=-1.0).then_inc(w_exp, 1)

            def w_split(g, j):
                wait(act, n_mm, GB * g)
                high(h1_h[:, j, :], elu_out[j % 4], w_elu, KH * g + j + 1, w_high)

            def nn(g, j):
                wait(act, o_mm, 2 * g)
                high(wh2_h[:, j, :], bank_of("N", j)[:, 0:O2], n_mm, GB * g + j + 1, n_high)

            def ft(g, j):
                high(rows2[:], bank_of("fT")[:, 0:P], ft_mm, g + 1, ft_high)

            def p2(g, j):
                high(p2_h[:].rearrange("p b n -> p (b n)"), bank_of("P2")[:], p2_mm, g + 1, p2_high)

            def o_first(g, j):
                wait(act, o_mm, 2 * g + j + 1)
                wait(act, o_elu, 2 * g + j - 1)
                act.activation(o_exp[j], bank_of("O", j)[:], ACT.Relu, scale=-1.0).then_inc(o_neg, 1)

            def o_second(g, j):
                wait(act, o_neg, 2 * g + j + 1)
                act.activation(o_exp[j], o_exp[j], ACT.Exp, scale=-1.0).then_inc(o_exp_done, 1)

            def turned_o(g, j):
                high(o_h[:, j, :], bank_of("oT", j)[:], ot_mm, KO * g + j + 1, ot_high)

            def m(g, j):
                wait(act, m_mm, KD * g + j + 1)
                wait(act, m_low, KD * g + j - 1)
                act.activation(m_f[j], bank_of("M", j)[:], ACT.Relu, bias=b1_col[:, j:j + 1]).then_inc(m_relu, 1)

            def m_split(g, j):
                wait(act, f_mm, min(g + 3, NG) if isinstance(g, int) else g + 3)
                high(blk_h[:, j, :], m_f[j], m_relu, KD * g + j + 1, m_high)

            def y_norm_op(g, j):
                wait(act, y_nbias, g + 1)
                for b in range(GB):
                    act.activation(y[:, b, :], y[:, b, :], ACT.Identity, bias=nbias2[:, b:b + 1],
                                   scale=rstd2[:, b:b + 1]).then_inc(y_norm, 1)

            def wheads_split():
                act.wait_ge(wheads_loaded, 16)
                act.activation(wh_h[:], wheads_f, ACT.Copy).then_inc(wheads_high, 1)

            def late_split():
                act.wait_ge(wout_loaded, 16)
                act.activation(wo_h[:, :, 0:O2], wout_f, ACT.Copy).then_inc(late_high, 1)
                act.wait_ge(ffn_loaded, 32)
                act.activation(w1_h[:], ffn_f[:, 0:2, :], ACT.Copy).then_inc(late_high, 1)
                act.activation(w2_h[:], ffn_f[:, 2:4, :], ACT.Copy).then_inc(late_high, 1)

            def staging_free():
                act.wait_ge(vec_loaded, 64)
                act.wait_ge(late_low, 3)
                act.wait_ge(woa_ready, 1)

            all_steps(act, ACT_ORDER, {
                "LNr": ln_relu_op, "hTh": ht, "Fh": f, "Su": s, "Ru": r, "PTh": pt, "Gh": gg, "Wn": w_first,
                "We": w_second, "Wh": w_split, "Nh": nn, "fTh": ft, "P2h": p2, "On": o_first, "Oe": o_second,
                "oTh": turned_o, "Mr": m, "Mh": m_split, "Yn": y_norm_op,
                "Se": lambda g, j: exps(j, s_shift, GB * g + j + 1, s_exp),
                "Re": lambda g, j: exps(GB, r_shift, g + 1, r_exp)},
                {(-1, "Fh"): wheads_split, (0, "Wn0"): late_split, (1, "Ru"): staging_free})

        @block.vector
        def _(dve):
            def low(dst, psum, high, ready, n, done):
                wait(dve, ready, n)
                dve.tensor_tensor(dst, psum, high.bitcast(F32), ALU.subtract).then_inc(done, 1)

            def stats(src, st, mean, diff, ve, g, s_stats, s_step, s_var):
                for b in range(GB):
                    dve.bn_stats(st[:, b, :], src[:, b, :]).then_inc(s_stats, 1)
                wait(dve, s_stats, GB * g + GB)
                dve.tensor_tensor(diff[:], st[:, :, 1], st[:, :, 4], ALU.subtract).then_inc(s_step, 1)
                dve.tensor_tensor(mean[:], st[:, :, 1], st[:, :, 4], ALU.add).then_inc(s_step, 1)
                dve.scalar_tensor_tensor(ve[:], st[:, :, 2], F * LN_EPS, st[:, :, 5], ALU.add, ALU.add).then_inc(s_step, 1)
                wait(dve, s_step, 5 * g + 3)
                dve.scalar_tensor_tensor(diff[:], diff[:], 0.25, diff[:], ALU.mult, ALU.mult).then_inc(s_step, 1)
                dve.tensor_scalar(mean[:], mean[:], 0.5, None, ALU.mult).then_inc(s_step, 1)
                wait(dve, s_step, 5 * g + 5)
                dve.scalar_tensor_tensor(ve[:], ve[:], 1.0 / F, diff[:], ALU.mult, ALU.add).then_inc(s_var, 1)

            def ln_stats_op(g, j):
                wait(dve, x_in_ready, 16 * g + 16)
                wait(dve, ln_rstd, g)
                stats(x_in, st1, mean1, diff1, ve1, g, ln_stats, ln_step, ln_var)

            def ln_bias_op(g, j):
                wait(dve, ln_rstd, g + 1)
                wait(dve, ln_relu, GB * g)
                dve.scalar_tensor_tensor(nbias1[:], mean1[:], -1.0, rstd1[:], ALU.mult, ALU.mult).then_inc(ln_bias, 1)

            def ht(g, j):
                low(blk_l[:, j, :], bank_of("hT", j)[:], blk_h[:, j, :], ht_high, KF * g + j + 1, ht_low)

            def h_split(g, j):
                wait(dve, ln_relu, GB * g + GB)
                wait(dve, g_mm, GB * KF * g)
                wait(dve, h_low, g)
                dve.tensor_copy(h_h[:], h_f[:]).then_inc(h_high, 1)

            def f(g, j):
                lows = slice(PART, 2 * PART)
                low(rows[lows, :], bank_of("F")[lows, :], rows[lows, :], f_high, g + 1, f_low)

            def leaky(tile, psum, buf, ready, done, n):
                wait(dve, ready, n)
                dve.tensor_tensor(z[:, tile, :, :].rearrange("p a m -> p (a m)"), psum[:],
                                  buf[:].rearrange("p a m -> p (a m)"), ALU.max).then_inc(done, 1)

            def row_max(tile, ready, done, n):
                wait(dve, ready, n)
                dve.tensor_reduce(zmax[:, tile, :], z[:, tile, :, :], AX_X, ALU.max).then_inc(done, 1)

            def sums(tile, ready, s_s, s_i, n):
                wait(dve, ready, n)
                dve.tensor_reduce(zsum[:, tile, :], z[:, tile, :, :], AX_X, ALU.add).then_inc(s_s, 1)
                wait(dve, s_s, n)
                dve.reciprocal(zinv[:, tile, :], zsum[:, tile, :]).then_inc(s_i, 1)

            def s_leaky_op(g, j):
                wait(dve, pt_mm, GB * (g - 1) + j + 1)
                leaky(j, bank_of("S", j), slope[j % 2], s_slope, s_leaky, GB * g + j + 1)

            def r_leaky_op(g, j):
                wait(dve, p2_mm, g)
                leaky(GB, bank_of("R"), slope[2], r_slope, r_leaky, g + 1)

            def pt(g, j):
                low(pt_l[:, j % 2, :], bank_of("PT", j)[:], pt_h[:, j % 2, :], pt_high, GB * g + j + 1, pt_low)

            def gg(g, j):
                b, k = divmod(j, KF)
                low(g_l[:, k, :, b, :], bank_of("G", j)[:].rearrange("p (h n) -> p h n", h=H), g_h[:, k, :, b, :],
                    g_high, GB * KF * g + j + 1, g_low)

            def w(g, j):
                wait(dve, w_exp, KH * g + j + 1)
                wait(dve, w_low, KH * g + j - 3)
                dve.scalar_tensor_tensor(elu_out[j % 4], elu_exp[j % 2], -1.0, bank_of("W", j)[:], ALU.add, ALU.max
                                         ).then_inc(w_elu, 1)

            def nn(g, j):
                psum = bank_of("N", j)
                wait(dve, ft_mm, g)
                low(wh2_l[:, j, :], psum[:, 0:O2], wh2_h[:, j, :], n_high, GB * g + j + 1, n_part)
                cols = f2n[:, 0:2 * PART].rearrange("p (r c) -> p r c", r=2)[:, :, j:j + GB + 1:GB]
                dve.tensor_copy(cols, psum[:, O2:NAUG].unsqueeze(1).to_broadcast([P, 2, 2])).then_inc(n_low, 1)

            def ft(g, j):
                lows = slice(PART, 2 * PART)
                low(rows2[lows, :], bank_of("fT")[lows, 0:P], rows2[lows, :], ft_high, g + 1, ft_low)

            def p2(g, j):
                low(p2_l[:].rearrange("p b n -> p (b n)"), bank_of("P2")[:], p2_h[:].rearrange("p b n -> p (b n)"),
                    p2_high, g + 1, p2_low)

            def o(g, j):
                wait(dve, o_exp_done, 2 * g + j + 1)
                wait(dve, ot_mm, KO * g)
                wait(dve, o_bias, 2 * g)
                dve.scalar_tensor_tensor(o_f[j].rearrange("p b c -> p (b c)"), o_exp[j], -1.0, bank_of("O", j)[:],
                                         ALU.add, ALU.max).then_inc(o_elu, 1)

            def turned_o(g, j):
                low(o_l[:, j, :], bank_of("oT", j)[:], o_h[:, j, :], ot_high, KO * g + j + 1, ot_low)

            def m(g, j):
                low(blk_l[:, j, :], m_f[j], blk_h[:, j, :], m_high, KD * g + j + 1, m_low)

            def yy(g, j):
                wait(dve, y_mm, 2 * g + j + 1)
                wait(dve, o_bias, 2 * g + j + 1)
                pair = y[:, 2 * j:2 * j + 2, :].rearrange("p b c -> p (b c)")
                dve.tensor_tensor(pair, bank_of("Y", j)[:], pair, ALU.add).then_inc(y_sum, 1)

            def y_stats_op(g, j):
                wait(dve, y_sum, 2 * g + 2)
                stats(y, st2, mean2, diff2, ve2, g, y_stats, y_step, y_var)

            def y_nbias_op(g, j):
                wait(dve, y_rstd, g + 1)
                dve.scalar_tensor_tensor(nbias2[:], mean2[:], -1.0, rstd2[:], ALU.mult, ALU.mult).then_inc(y_nbias, 1)

            def y_last(g, j):
                wait(dve, y_gamma, g + 1)
                wait(dve, xb_ready, g + 1)
                dve.tensor_tensor(y[:], y[:], x_res[:], ALU.add).then_inc(y_done, 1)

            dve.wait_ge(patterns, 4)
            dve.tensor_copy(ident_b[:], ident[:]).then_inc(consts, 1)
            dve.tensor_reduce(picks[:], ident[:, 0:2 * PART].rearrange("p (a r) -> p a r", a=2)[:, :, 0:4 * H]
                              .rearrange("p a (l c) -> p c a l", l=2), AX_XY, ALU.add).then_inc(consts, 1)
            dve.wait_ge(consts, 2)
            for k, pick in enumerate((pick_f1, pick_f2)):
                dve.tensor_copy(pick[:], picks[:, k * H:(k + 1) * H].unsqueeze(2).to_broadcast([P, H, P])).then_inc(consts, 1)
            dve.memset(wa_f[:], 0.0).then_inc(wa_steps, 1)
            done = 1 + 2 * H * KF

            def wheads_a():
                dve.wait_ge(wheads_loaded, 16)
                dve.wait_ge(avec_loaded, 32)
                for h in range(H):
                    for k in range(KF):
                        for half in range(2):
                            a = avec_f[h // 2][:, 2 * (h % 2) + half, :]
                            dve.wait_ge(wa_steps, max(1, 2 * (h * KF + k) + half))
                            dve.tensor_tensor_reduce(junk[half], wheads_f[:, h * KF + k, :], a, 1.0, 0.0, ALU.mult, ALU.add,
                                                     wa_f[:, k, h + H * half:h + H * half + 1]).then_inc(wa_steps, 1)
                dve.wait_ge(wa_steps, done)
                dve.tensor_copy(wa_f[:, :, PART:PART + 2 * H], wa_f[:, :, 0:2 * H]).then_inc(wa_steps, 1)
                dve.wait_ge(wa_steps, done + 1)
                dve.tensor_copy(wa_h[:], wa_f[:]).then_inc(wa_steps, 1)
                dve.wait_ge(wa_steps, done + 2)
                dve.tensor_copy(wa_hl[:], wa_h[:]).then_inc(wa_steps, 1)
                dve.wait_ge(wa_steps, done + 3)
                for first in (0, PART):
                    part = slice(first, first + 2 * H)
                    dve.tensor_tensor(wa_hl[:, :, first + 2 * H:first + 4 * H], wa_f[:, :, part], wa_h[:, :, part].bitcast(F32),
                                      ALU.subtract).then_inc(wa_ready, 1)
                mask_from_adj()

            def mask_from_adj():
                dve.wait_ge(adj_loaded, 16)
                dve.tensor_scalar(z[:, GB, 1, :], z[:, GB, 0, :].bitcast(I32), 0, 1.0, ALU.is_gt, ALU.subtract).then_inc(consts, 1)
                dve.wait_ge(consts, 5)
                dve.tensor_scalar(mask[:], z[:, GB, 1, :].unsqueeze(1).to_broadcast([P, GB, P]), MASKED, None, ALU.mult
                                  ).then_inc(mask_ready, 1)

            def wout_a():
                dve.wait_ge(wout_loaded, 16)
                dve.wait_ge(aout_loaded, 16)
                n = done + 3
                for k in range(KH):
                    for half in range(2):
                        dve.wait_ge(wa_steps, n + 2 * k + half - 1)
                        dve.tensor_tensor_reduce(junk2[half], wout_f[:, k, :], aout_f[:, half * O2:(half + 1) * O2],
                                                 1.0, 0.0, ALU.mult, ALU.add, wo_a[:, k, half:half + 1]).then_inc(wa_steps, 1)
                n += 2 * KH
                dve.wait_ge(wa_steps, n)
                dve.tensor_copy(wo_h[:, :, O2:NAUG], wo_a[:]).then_inc(wa_steps, 1)
                dve.wait_ge(wa_steps, n + 1)
                dve.tensor_tensor(wo_l[:, :, O2:NAUG], wo_a[:], wo_h[:, :, O2:NAUG].bitcast(F32), ALU.subtract).then_inc(woa_ready, 1)

            all_steps(dve, DVE_ORDER, {
                "LNs": ln_stats_op, "LNb": ln_bias_op, "hTl": ht, "Hh": h_split, "Fl": f, "PTl": pt, "Gl": gg, "Wv": w,
                "Nl": nn, "fTl": ft, "P2l": p2, "Ov": o, "oTl": turned_o, "Ml": m, "Yb": yy, "Yst": y_stats_op, "Ynb": y_nbias_op,
                "Yo": y_last, "Sl": s_leaky_op, "Rl": r_leaky_op,
                "Sm": lambda g, j: row_max(j, s_leaky, s_max, GB * g + j + 1),
                "Rm": lambda g, j: row_max(GB, r_leaky, r_max, g + 1),
                "Sr": lambda g, j: sums(j, s_exp, s_sum, s_inv, GB * g + j + 1),
                "Rr": lambda g, j: sums(GB, r_exp, r_sum, r_inv, g + 1)},
                {(-1, "Fl"): wheads_a, (0, "Wv0"): wout_a})

        @block.gpsimd
        def _(pool):
            def low(dst, value, high, ready, n, done):
                wait(pool, ready, n)
                pool.tensor_tensor(dst, value, high.bitcast(F32), ALU.subtract).then_inc(done, 1)

            def inverse_root(dst, var, ready, n, done):
                wait(pool, ready, n)
                pool.tensor_tensor(dst[:], var[:], half_power[:], ALU.pow).then_inc(done, 1)

            def ln_root(g, j):
                wait(pool, ln_relu, GB * g)
                inverse_root(rstd1, ve1, ln_var, g + 1, ln_rstd)

            def y_root(g, j):
                wait(pool, y_norm, GB * g)
                inverse_root(rstd2, ve2, y_var, g + 1, y_rstd)

            def h_split(g, j):
                low(h_l[:], h_f[:], h_h[:], h_high, g + 1, h_low)

            def by_block(tile, op, factors, ready, n, done):
                wait(pool, ready, n)
                pool.tensor_tensor(z[:, tile, :, :], z[:, tile, :, :],
                                   factors[:, tile, :].unsqueeze(2).to_broadcast([P, GB, P]), op).then_inc(done, 1)

            def w(g, j):
                low(h1_l[:, j, :], elu_out[j % 4], h1_h[:, j, :], w_high, KH * g + j + 1, w_low)

            def o_plus_b2(g, j):
                wait(pool, o_elu, 2 * g + j + 1)
                wait(pool, out_stored, 16 * g)
                pool.tensor_tensor(y[:, 2 * j:2 * j + 2, :], o_f[j], b2_bc[:].unsqueeze(1).to_broadcast([P, 2, O2]), ALU.add
                                   ).then_inc(o_bias, 1)

            def residual(g, j):
                wait(pool, x_res_ready, 16 * g + 16)
                pool.tensor_tensor(x_res[:], x_res[:], beta_bc[:].unsqueeze(1).to_broadcast([P, GB, O2]), ALU.add
                                   ).then_inc(xb_ready, 1)

            def y_scale(g, j):
                wait(pool, y_norm, GB * g + GB)
                pool.tensor_tensor(y[:], y[:], gamma_bc[:].unsqueeze(1).to_broadcast([P, GB, O2]), ALU.mult
                                   ).then_inc(y_gamma, 1)

            pool.memset(half_power[:], -0.5).then_inc(patterns, 1)
            pool.memset(f2n[:], 0.0).then_inc(patterns, 1)
            pool.memset(ident[:], 0.0).then_inc(patterns, 1)
            pool.wait_ge(patterns, 3)
            pool.affine_select(out=ident[:], in_=ident[:], compare_op=ALU.not_equal, fill=1.0, base=0,
                               pattern=[[-1, P]], channel_multiplier=1).then_inc(patterns, 1)

            def wheads_split():
                pool.wait_ge(wheads_high, 1)
                pool.tensor_tensor(wh_l[:], wheads_f, wh_h[:].bitcast(F32), ALU.subtract).then_inc(wheads_low, 1)

            def late_split():
                for k, (dst, src, hi) in enumerate((
                        (wo_l[:, :, 0:O2], wout_f, wo_h[:, :, 0:O2]), (w1_l[:], ffn_f[:, 0:2, :], w1_h[:]),
                        (w2_l[:], ffn_f[:, 2:4, :], w2_h[:]))):
                    pool.wait_ge(late_high, k + 1)
                    pool.tensor_tensor(dst, src, hi.bitcast(F32), ALU.subtract).then_inc(late_low, 1)

            def rows_loaded():
                pool.wait_ge(vec_loaded, 64)
                pool.wait_ge(wa_ready, 2)

            all_steps(pool, POOL_ORDER, {
                "LNp": ln_root, "Hl": h_split, "Wl": w, "ob": o_plus_b2, "xb": residual, "Yp": y_root, "Yg": y_scale,
                "Ss": lambda g, j: by_block(j, ALU.subtract, zmax, s_max, GB * g + j + 1, s_shift),
                "Sp": lambda g, j: by_block(j, ALU.mult, zinv, s_inv, GB * g + j + 1, s_prob),
                "Rs": lambda g, j: by_block(GB, ALU.subtract, zmax, r_max, g + 1, r_shift),
                "Rp": lambda g, j: by_block(GB, ALU.mult, zinv, r_inv, g + 1, r_prob)},
                {(-1, "Ss0"): wheads_split, (0, "Wl0"): late_split, (1, "Rs"): rows_loaded})


_INS = ["x", "adj", "L0_gnn_W_heads", "L0_gnn_a_heads", "L0_gnn_W_out", "L0_gnn_a_out", "L0_gnn_w1", "L0_gnn_b1",
        "L0_gnn_w2", "L0_gnn_b2", "L0_gnn_ln_gamma", "L0_gnn_ln_beta"]


def kernel(**inputs):
    import concourse.bacc as _bacc
    from concourse.bass_utils import run_bass_kernel_spmd as _run

    nc = _bacc.Bacc("TRN2", target_bir_lowering=False, num_devices=1, dynamic_dma_scratch_size=1024)
    arrays, args = {}, []
    for name in _INS:
        a = np.ascontiguousarray(inputs[name])
        arrays[f"in_{name}_dram"] = a
        args.append(nc.dram_tensor(f"in_{name}_dram", a.shape, mybir.dt.from_np(a.dtype), kind="ExternalInput").ap())
    shape = inputs["x"].shape
    out = nc.dram_tensor("out_dram", shape, F32, kind="ExternalOutput").ap()
    gat_kernel(nc, *args, out)
    r = _run(nc, [arrays], core_ids=[0])
    return r.results[0]["out_dram"]
```

```python
from contextlib import ExitStack

import numpy as np

import concourse.bass as bass
from concourse import mybir
from concourse.alu_op_type import AluOpType as ALU

F32 = mybir.dt.float32
F32R = mybir.dt.float32r
BF16 = mybir.dt.bfloat16
I32 = mybir.dt.int32
ACT = mybir.ActivationFunctionType
AX_X = mybir.AxisListType.X
AX_XY = mybir.AxisListType.XY

P = 128
GB = 4
GN = GB * P
LEAKY = 0.01
LN_EPS = 1e-5
MASKED = 2.0 ** 127
PART = 32

PE_START = """
    warm0:27 hT0:0 hT1:0 warm0:19 F:0 warm0:6 S0:0 S1:0 S2:0 S3:0 warm0:7 hT0:1 hT1:1 warm0:6 PT0:0 warm0:3 F:1
    G0:0 G1:0 PT1:0 S0:1 S1:1 PT2:0 G2:0 G3:0 PT3:0 G4:0 G5:0 G6:0 G7:0 S2:1 S3:1 W0:0 W1:0 W2:0 W3:0 PT0:1 W4:0
    W5:0 W6:0 warm6:4 W7:0 PT1:1 G0:1 G1:1 G2:1 G3:1 N0:0 N1:0
""".split()
PE_STEP = """
    PT2@0 PT3@6 N2@4 N3@3 G4@1 G5@2 G6@7 fT@0 G7@6 R@4 W0@0 hT0@7 hT1@3 W1@1 W2@5 F@3 W3@7 P2@6 S0@2 S1@3 O0@6
    O1@5 S2@4 W4@3 W5@1 oT0@6 oT1@7 W6@0 S3@2 PT0@4 M0@5 M1@7 G0@6 W7@3 PT1@5 G1@4 Y0@1 G2@7 Y1@2 G3@5 N0@1 N1@2
""".split()
PE_END = """
    PT2:1 PT3:1 N2:0 N3:0 G4:1 G5:1 fT:0 G6:1 G7:1 R:0 W0:1 W1:1 W2:1 W3:1 W4:1 W5:1 W6:1 P2:0 W7:1 warm2:3 O0:0
    O1:0 warm2:7 N0:1 N1:1 N2:1 oT0:0 oT1:0 N3:1 M0:0 fT:1 warm1:3 R:1 M1:0 warm2:9 Y0:0 Y1:0 P2:1 warm3:6 O0:1
    O1:1 warm3:12 oT0:1 oT1:1 warm3:7 M0:1 M1:1 warm3:9 Y0:1 Y1:1
""".split()
ACT_START = """
    LNr:0 hTh0:0 whH:0 hTh1:0 Fh:0 woH:0 Su0:0 Su1:0 Su2:0 LNr:1 Se0:0 hTh0:1 Su3:0 Se1:0 hTh1:1 PTh0:0 Se2:0
    Fh:1 Gh0:0 Se3:0 PTh1:0 Gh1:0 Su0:1 PTh2:0 Gh2:0 Gh3:0 PTh3:0 Su1:1 Gh4:0 Gh5:0 Gh6:0 Gh7:0 Su2:1 Se0:1
    Su3:1 Wn0:0 We0:0 Se1:1 Wn1:0 We1:0 Wn2:0 Wh0:0 Wn3:0 We2:0 We3:0 Wh1:0 Wh2:0 PTh0:1 Wn4:0 Wn5:0 We4:0 We5:0
    Wh3:0 Wn6:0 Wh4:0 We6:0 Wh5:0 PTh1:1 Wn7:0 We7:0 Wh6:0 Gh0:1 Wh7:0 Se2:1 Gh1:1 Se3:1 Nh0:0 Gh2:1 PTh2:1
    PTh3:1 Gh3:1 wfH:0
""".split()
ACT_STEP = """
    Nh1 Nh2 Nh3 Gh4 Gh5 Gh6 fTh Gh7 LNr Ru Wn0 hTh0 hTh1 We0 Re Wn1 We1 Fh Wn2 Wh0 P2h We2 Wn3 Su0 Su1 On0 On1
    Oe0 Su2 Oe1 We3 Se0 Wn4 Wh1 oTh0 Wh2 oTh1 Se1 We4 Wh3 PTh0 Su3 Wn5 Mr0 We5 Mr1 Mh0 Mh1 Wh4 PTh1 Wn6 Wh5 We6
    Wn7 We7 Wh6 Wh7 Gh0 Gh1 Se2 Se3 Gh2 Nh0 Gh3 Yn PTh2 PTh3
""".split()
ACT_END = """
    Nh1:0 Nh2:0 Nh3:0 Gh4:1 Gh5:1 fTh:0 Gh6:1 Gh7:1 Ru:0 Wn0:1 We0:1 Wn1:1 Re:0 We1:1 Wn2:1 Wh0:1 We2:1 Wh1:1
    Wn3:1 Wn4:1 We3:1 We4:1 Wh2:1 Wn5:1 Wh3:1 We5:1 P2h:0 Wn6:1 Wh4:1 Wh5:1 We6:1 Wn7:1 We7:1 Wh6:1 Wh7:1 On0:0
    Nh0:1 Oe0:0 Nh1:1 On1:0 Oe1:0 oTh0:0 oTh1:0 Nh2:1 Nh3:1 fTh:1 Mr0:0 Mh0:0 Ru:1 Mr1:0 Mh1:0 Re:1 P2h:1 On0:1
    On1:1 Oe0:1 Oe1:1 Yn:0 oTh0:1 oTh1:1 Mr0:1 Mh0:1 Mr1:1 Mh1:1 Yn:1
""".split()
DVE_START = """
    LNs:0 WA0:0 LNb:0 WA1:0 WA2:0 MK:0 WA3:0 hTl0:0 WAf:0 hTl1:0 LNs:1 Fl:0 Hh:0 OA0:0 Sl0:0 LNb:1 Sl1:0 Sm0:0
    Sm1:0 Sl2:0 Sm2:0 Sr0:0 hTl0:1 Sl3:0 Sr1:0 hTl1:1 PTl0:0 Sm3:0 Sr2:0 Fl:1 Gl0:0 Sr3:0 PTl1:0 Sl0:1 Gl1:0
    PTl2:0 Gl2:0 Gl3:0 PTl3:0 Sm0:1 Gl4:0 Gl5:0 Gl6:0 Gl7:0 Sl1:1 Sm1:1 Sl2:1 Sm2:1 Sr0:1 Wv0:0 Hh:1 Wv1:0 OA1:0
    Wv2:0 Sr1:1 Wv3:0 OA2:0 Wv4:0 Wv5:0 PTl0:1 OA3:0 Wv6:0 PTl1:1 OAf:0 Wv7:0 Sl3:1 Sm3:1 Sr2:1 Gl0:1 Sr3:1
    Gl1:1 Gl2:1 PTl2:1 Nl0:0 PTl3:1 Gl3:1 Nl1:0 Nl2:0
""".split()
DVE_STEP = """
    LNs Nl3 Gl4 Gl5 LNb fTl Gl6 Gl7 Rl Rm hTl0 hTl1 Wv0 Rr Hh Fl Wv1 P2l Wv2 Sl0 Sl1 Sm0 Sm1 Ov0 Ov1 Wv3 Sr0 Sl2
    oTl0 oTl1 Sr1 Wv4 PTl0 Sm2 Sl3 Wv5 Ml0 Ml1 PTl1 Sm3 Wv6 Yb0 Wv7 Yb1 Yst Sr2 Ynb Sr3 Gl0 Gl1 Nl0 Gl2 PTl2 Gl3
    Nl1 PTl3 Yo Nl2
""".split()
DVE_END = """
    Nl3:0 Gl4:1 Gl5:1 fTl:0 Gl6:1 Gl7:1 Rl:0 Rm:0 Wv0:1 Rr:0 Wv1:1 Wv2:1 Wv3:1 Wv4:1 Wv5:1 P2l:0 Wv6:1 Wv7:1
    Nl0:1 Ov0:0 Nl1:1 Ov1:0 oTl0:0 oTl1:0 Nl2:1 Nl3:1 fTl:1 Ml0:0 Rl:1 Rm:1 Ml1:0 Rr:1 Yb0:0 Yb1:0 P2l:1 Yst:0
    Ynb:0 Ov0:1 Ov1:1 oTl0:1 oTl1:1 Yo:0 Ml0:1 Ml1:1 Yb0:1 Yb1:1 Yst:1 Ynb:1 Yo:1
""".split()
POOL_START = """
    LNp:0 whL:0 LNp:1 Hl:0 Ss0:0 Ss1:0 Sp0:0 Ss2:0 Sp1:0 Ss3:0 Sp2:0 Sp3:0 woL:0 Ss0:1 Ss1:1 Ss2:1 Sp0:1 Hl:1
    Wl0:0 Sp1:1 Wl1:0 Wl2:0 Wl3:0 Wl4:0 Wl5:0 Wl6:0 Wl7:0 Ss3:1 Sp2:1 Sp3:1 wfL:0
""".split()
POOL_STEP = """
    LNp xb Rs Rp Wl0 Hl Ss0 Ss1 ob0 Sp0 Wl1 Wl2 Sp1 Wl3 ob1 Ss2 Wl4 Wl5 Ss3 Wl6 Wl7 Yp Sp2 Sp3 Yg
""".split()
POOL_END = """
    xb:0 Rs:0 Wl0:1 Rp:0 Wl1:1 Wl2:1 Wl3:1 Wl4:1 Wl5:1 Wl6:1 Wl7:1 ob0:0 Rs:1 ob1:0 Rp:1 Yp:0 xb:1 Yg:0 ob0:1
    ob1:1 Yp:1 Yg:1
""".split()
AHEAD = """
    hT0 hT1 F S0 S1 S2 S3 PT0 G0 PT1 G1 G2 G3 LNr hTh0 hTh1 Fh Su0 Su1 Su2 Se0 Se1 PTh0 Su3 PTh1 Gh0 Gh1 Se2 Se3
    Gh2 Gh3 PTh2 PTh3 LNs LNb hTl0 hTl1 Hh Fl Sl0 Sl1 Sm0 Sm1 Sr0 Sl2 Sr1 PTl0 Sm2 Sl3 PTl1 Sm3 Sr2 Sr3 Gl0 Gl1
    Gl2 PTl2 Gl3 PTl3 LNp Hl Ss0 Ss1 Sp0 Sp1 Ss2 Ss3 Sp2 Sp3
""".split()
BEHIND = """
    N2 N3 fT R P2 O0 O1 oT0 oT1 M0 M1 Y0 Y1 Nh1 Nh2 Nh3 fTh Ru Re P2h On0 On1 Oe0 Oe1 oTh0 oTh1 Mr0 Mr1 Mh0 Mh1
    Yn Nl3 fTl Rl Rm Rr P2l Ov0 Ov1 oTl0 oTl1 Ml0 Ml1 Yb0 Yb1 Yst Ynb Yo xb Rs Rp ob0 ob1 Yp Yg
""".split()
BANK = {op.split("@")[0]: int(op.split("@")[1]) for op in PE_STEP}
BANK.update(warm0=0, warm1=1, warm2=2, warm3=3, warm6=6)
PE_STEP = [op.split("@")[0] for op in PE_STEP]


def with_groups(order, first):
    pairs = [(item.split(":")[0], int(item.split(":")[1])) for item in order]
    return [(op, n if "warm" in op else first + n) for op, n in pairs]


def group_of(op, i):
    return i + 1 if op in AHEAD else i - 1 if op in BEHIND else i


def split_name(op):
    if op in ("P2", "P2h", "P2l"):
        return op, 0
    return (op[:-1], int(op[-1])) if op[-1].isdigit() else (op, 0)


def gat_kernel(nc: bass.Bass, x, adj, W_heads, a_heads, W_out, a_out, w1, b1, w2, b2, ln_gamma, ln_beta, out):
    B, N, F = x.shape
    H = W_heads.shape[0]
    O1 = W_heads.shape[2]
    O2 = W_out.shape[1]
    D = w1.shape[1]
    NG = B // GB
    KF = F // P
    KH = H * O1 // P
    KO = O2 // P
    KD = D // P
    NAUG = O2 + 2
    assert N == P and H == GB and F == O1 == O2 == D == 256 and B % GB == 0 and NG % 2 == 0 and NG >= 6

    x_g = x.rearrange("(g b) n f -> g n b f", b=GB)
    out_g = out.rearrange("(g b) n f -> g n b f", b=GB)

    with ExitStack() as ctx:
        def sb(name, shape, dt=F32):
            return ctx.enter_context(nc.sbuf_tensor(name, shape, dt))

        def sem(name):
            return ctx.enter_context(nc.semaphore(name))

        bank = [ctx.enter_context(nc.psum_tensor(f"bank{i}", [P, GN], F32)) for i in range(8)]

        def bank_of(kind, j=None):
            return bank[BANK[kind if j is None else f"{kind}{j}"]]

        ident = sb("ident", [P, P])
        ident_b = sb("ident_b", [P, P], BF16)
        mask = sb("mask", [P, GB, P], BF16)
        pick_f1 = sb("pick_f1", [P, GB, P], F32R)
        pick_f2 = sb("pick_f2", [P, GB, P], F32R)
        picks = sb("picks", [P, 2 * H])
        half_power = sb("half_power", [P, GB])
        wa_f = sb("wa_f", [P, KF, P])
        wa_h = sb("wa_h", [P, KF, P], F32R)
        wa_hl = sb("wa_hl", [P, KF, P], F32R)
        wh_h, wh_l = (sb(f"wheads_{t}", [P, H * KF, O1], F32R) for t in "hl")
        wo_a = sb("wo_a", [P, KH, 2])
        wo_h, wo_l = (sb(f"wout_{t}", [P, KH, NAUG], F32R) for t in "hl")
        w1_h, w1_l = (sb(f"w1_{t}", [P, KO, D], F32R) for t in "hl")
        w2_h, w2_l = (sb(f"w2_{t}", [P, KD, O2], F32R) for t in "hl")
        b1_col = sb("b1_col", [P, KD])
        b2_bc, gamma_bc, beta_bc = (sb(f"{t}_bc", [P, O2]) for t in ("b2", "gamma", "beta"))

        scratch = sb("scratch", [P, 12, GN])
        elu_out = [scratch[:, k, :] for k in range(4)]
        elu_exp = [scratch[:, 4 + k, :] for k in range(2)]
        o_exp = [scratch[:, 6 + k, :] for k in range(2)]
        o_f = [scratch[:, 8 + k, :].rearrange("p (b c) -> p b c", b=2) for k in range(2)]
        m_f = [scratch[:, 10 + k, :] for k in range(2)]
        x_in = sb("x_in", [P, GB, F])
        x_res = sb("x_res", [P, GB, F])
        y = sb("y", [P, GB, O2])
        h_f = sb("h_f", [P, GB, F])
        h_h, h_l = (sb(f"h_{t}", [P, GB, F], F32R) for t in "hl")
        blk_h, blk_l = (sb(f"blk_{t}", [P, 2, GN], F32R) for t in "hl")
        rows = sb("rows", [P, GN], F32R)
        rows2 = sb("rows2", [P, P], F32R)
        f2n = sb("f2n", [P, P])
        slope = [sb(f"slope{k}", [P, GB, P]) for k in range(3)]
        z = sb("z", [P, GB + 1, GB, P])
        zmax = sb("zmax", [P, GB + 1, GB])
        zsum = sb("zsum", [P, GB + 1, GB])
        zinv = sb("zinv", [P, GB + 1, GB])
        pt_h, pt_l = (sb(f"pt_{t}", [P, 2, GN], F32R) for t in "hl")
        p2_h, p2_l = (sb(f"p2_{t}", [P, GB, P], F32R) for t in "hl")
        g_h, g_l = (sb(f"g_{t}", [P, KF, H, GB, P], F32R) for t in "hl")
        h1_h, h1_l = (sb(f"h1_{t}", [P, KH, GN], F32R) for t in "hl")
        wh2_h, wh2_l = (sb(f"wh2_{t}", [P, GB, O2], F32R) for t in "hl")
        o_h, o_l = (sb(f"o_{t}", [P, KO, GN], F32R) for t in "hl")
        st1, st2 = (sb(f"st{k}", [P, GB, 6]) for k in (1, 2))
        mean1, mean2 = (sb(f"mean{k}", [P, GB]) for k in (1, 2))
        diff1, diff2 = (sb(f"diff{k}", [P, GB]) for k in (1, 2))
        ve1, ve2 = (sb(f"ve{k}", [P, GB]) for k in (1, 2))
        rstd1, rstd2 = (sb(f"rstd{k}", [P, GB]) for k in (1, 2))
        nbias1, nbias2 = (sb(f"nbias{k}", [P, GB]) for k in (1, 2))

        wheads_f = scratch[:, 0:4, :].rearrange("p a c -> p (a c)").rearrange("p (k o) -> p k o", o=O1)
        ffn_f = scratch[:, 6:8, :].rearrange("p a c -> p (a c)").rearrange("p (k o) -> p k o", o=O2)
        wout_f = scratch[:, 8:12, :].rearrange("p a c -> p (a c)").rearrange("p (k o) -> p k o", o=O2)
        aout_f = slope[2][:].rearrange("p b n -> p (b n)")
        junk = [slope[0][:, 2 * k:2 * k + 2, :].rearrange("p b n -> p (b n)") for k in range(2)]
        junk2 = [y[:, k, :] for k in range(2)]
        avec_f = [y, x_res]

        x_in_ready, x_res_ready, out_stored = sem("x_in_ready"), sem("x_res_ready"), sem("out_stored")
        wheads_loaded, avec_loaded = ([sem(f"{t}_loaded{k}") for k in range(2)] for t in ("wheads", "avec"))
        wout_loaded, ffn_loaded = (sem(f"{t}_loaded") for t in ("wout", "ffn"))
        aout_loaded, adj_loaded, vec_loaded = (sem(f"{t}_loaded") for t in ("aout", "adj", "vec"))
        patterns, consts, wa_steps, wa_ready, mask_ready, woa_ready = (
            sem(t) for t in ("patterns", "consts", "wa_steps", "wa_ready", "mask_ready", "woa_ready"))
        wheads_high, wheads_low, late_high, late_low = (sem(t) for t in ("wheads_high", "wheads_low", "late_high", "late_low"))
        ln_stats, ln_step, ln_var, ln_rstd, ln_bias, ln_relu = (
            sem(f"ln_{t}") for t in ("stats", "step", "var", "rstd", "bias", "relu"))
        h_high, h_low, ht_mm, ht_high, ht_low, f_mm, f_high, f_low = (
            sem(t) for t in ("h_high", "h_low", "ht_mm", "ht_high", "ht_low", "f_mm", "f_high", "f_low"))
        s_mm, s_slope, s_leaky, s_max, s_shift, s_exp, s_sum, s_inv, s_prob = (
            sem(f"s_{t}") for t in ("mm", "slope", "leaky", "max", "shift", "exp", "sum", "inv", "prob"))
        pt_mm, pt_high, pt_low, g_mm, g_high, g_low = (
            sem(t) for t in ("pt_mm", "pt_high", "pt_low", "g_mm", "g_high", "g_low"))
        w_mm, w_neg, w_exp, w_elu, w_high, w_low = (sem(f"w_{t}") for t in ("mm", "neg", "exp", "elu", "high", "low"))
        n_mm, n_high, n_part, n_low = (sem(f"n_{t}") for t in ("mm", "high", "part", "low"))
        ft_mm, ft_high, ft_low = (sem(f"ft_{t}") for t in ("mm", "high", "low"))
        r_mm, r_slope, r_leaky, r_max, r_shift, r_exp, r_sum, r_inv, r_prob = (
            sem(f"r_{t}") for t in ("mm", "slope", "leaky", "max", "shift", "exp", "sum", "inv", "prob"))
        p2_mm, p2_high, p2_low = (sem(f"p2_{t}") for t in ("mm", "high", "low"))
        o_mm, o_neg, o_exp_done, o_elu, o_bias = (sem(f"o_{t}") for t in ("mm", "neg", "exp_done", "elu", "bias"))
        ot_mm, ot_high, ot_low = (sem(f"ot_{t}") for t in ("mm", "high", "low"))
        m_mm, m_relu, m_high, m_low = (sem(f"m_{t}") for t in ("mm", "relu", "high", "low"))
        y_mm, y_sum, y_stats, y_step, y_var, y_rstd, y_nbias, y_norm, y_gamma, y_done, xb_ready = (
            sem(t) for t in ("y_mm", "y_sum", "y_stats", "y_step", "y_var", "y_rstd", "y_nbias", "y_norm", "y_gamma", "y_done", "xb_ready"))

        def wait(eng, s, n):
            if isinstance(n, int) and n <= 0:
                return
            eng.wait_ge(s, n)

        def first(g, j=0):
            return isinstance(g, int) and g == 0 and j == 0

        def residual_of(g):
            return x_in if isinstance(g, int) and g == NG - 1 else x_res

        def y_parts(g):
            if isinstance(g, int) and g == NG - 1:
                return [(0, 0, 2), (1, 2, 4)]
            return [(0, 0, GB)]

        def run(eng, start, order, end, ops, bank_user=None):
            def emit(op, group, user):
                if bank_user is not None:
                    bank_user[:] = user
                kind, j = split_name(op)
                ops[kind](group, j)

            def emit_all(items, before):
                for n, (op, g) in enumerate(items):
                    emit(op, g, [u for u in before + items[:n] if bank_user is not None and BANK[u[0]] == BANK[op]][-1:])

            def step(i):
                return [(op, group_of(op, i)) for op in order]

            emit_all(with_groups(start, 0) + step(1) + step(2), [])
            with eng.Fori(3, NG - 1, 2) as i0:
                for i in (i0, i0 + 1):
                    for op in order:
                        user = []
                        if bank_user is not None:
                            users = [u for u in order if BANK[u] == BANK[op]]
                            at = users.index(op)
                            user = [(users[at - 1], group_of(users[at - 1], i if at else i - 1))]
                        emit(op, group_of(op, i), user)
            emit_all(with_groups(end, NG - 2), step(NG - 2))

        block = ctx.enter_context(nc.Block())

        @block.sync
        def _(sp):
            sp.dma_start(x_in[:], x_g[0]).then_inc(x_in_ready, 16)
            for k in range(2):
                sp.dma_start(wheads_f[:, 2 * k * KF:2 * (k + 1) * KF, :],
                             W_heads[2 * k:2 * k + 2].rearrange("h (k p) o -> p (h k) o", p=P)).then_inc(wheads_loaded[k], 16)
                sp.dma_start(avec_f[k][:].rearrange("p (a c) f -> p a (c f)", a=2),
                             a_heads[2 * k:2 * k + 2, :].unsqueeze(0).to_broadcast([P, 2, 2 * O1])).then_inc(avec_loaded[k], 16)
            sp.dma_start(z[:, GB, 0, :].bitcast(I32), adj).then_inc(adj_loaded, 16)
            sp.wait_ge(ln_relu, GB)
            sp.dma_start(x_in[:], x_g[1]).then_inc(x_in_ready, 16)
            sp.dma_start(wout_f, W_out.rearrange("(k p) o -> p k o", p=P)).then_inc(wout_loaded, 16)
            sp.dma_start(aout_f, a_out.unsqueeze(0).to_broadcast([P, 2 * O2])).then_inc(aout_loaded, 16)
            for k, w in enumerate((w1, w2)):
                sp.dma_start(ffn_f[:, 2 * k:2 * k + 2, :], w.rearrange("(k p) o -> p k o", p=P)).then_inc(ffn_loaded, 16)
            for dst, src in ((b2_bc, b2), (gamma_bc, ln_gamma), (beta_bc, ln_beta)):
                sp.dma_start(dst[:], src.unsqueeze(0).to_broadcast([P, O2])).then_inc(vec_loaded, 16)
            with nc.allow_non_contiguous_dma("b1 as a column for each block"):
                sp.dma_start(b1_col[:], b1.rearrange("(k p) -> p k", p=P)).then_inc(vec_loaded, 16)
            sp.wait_ge(wa_ready, 2)
            sp.dma_start(x_res[:], x_g[0]).then_inc(x_res_ready, 16)
            sp.wait_ge(ln_relu, 2 * GB)
            sp.dma_start(x_in[:], x_g[2]).then_inc(x_in_ready, 16)

            def residual(g):
                sp.wait_ge(y_done, g)
                sp.dma_start(x_res[:], x_g[g]).then_inc(x_res_ready, 16)
                sp.dma_start(out_g[g - 1], y[:]).then_inc(out_stored, 16)

            with sp.Fori(1, NG - 2) as g:
                sp.wait_ge(ln_relu, GB * g + 2 * GB)
                sp.dma_start(x_in[:], x_g[g + 2]).then_inc(x_in_ready, 16)
                residual(g)
            residual(NG - 2)
            sp.wait_ge(y_done, NG - 1)
            sp.dma_start(out_g[NG - 2], y[:]).then_inc(out_stored, 16)
            for k, lo, hi in y_parts(NG - 1):
                sp.wait_ge(y_done, NG + k)
                sp.dma_start(out_g[NG - 1][:, lo:hi, :], y[:, lo:hi, :]).then_inc(out_stored, 16)
            sp.wait_ge(out_stored, 16 * (NG + 1))

        @block.tensor
        def _(pe):
            READ = {"PT": (pt_low, 4), "G": (g_low, 8), "W": (w_elu, 8), "N": (n_low, 4), "hT": (ht_low, 2),
                    "F": (f_low, 1), "S": (s_leaky, 4), "fT": (ft_low, 1), "R": (r_leaky, 1), "P2": (p2_low, 1),
                    "O": (o_elu, 2), "oT": (ot_low, 2), "M": (m_relu, 2), "Y": (y_sum, 2)}
            bank_user = []

            def wait_bank():
                for op, g in bank_user:
                    if "warm" in op:
                        continue
                    kind, j = split_name(op)
                    read, per_group = READ[kind]
                    wait(pe, read, per_group * g + j + 1)

            def three(psum, pairs):
                n = len(pairs)
                for k, (lh, ll, rh, rl) in enumerate(pairs):
                    pe.matmul(psum, lh, rh, start=(k == 0), stop=False)
                    pe.matmul(psum, lh, rl, start=False, stop=False)
                    last = pe.matmul(psum, ll, rh, start=False, stop=(k == n - 1))
                return last

            def transposed(g, j):
                wait(pe, ln_relu, GB * g + GB)
                wait_bank()
                for b in range(GB):
                    mm = pe.transpose(bank_of("hT", j)[:, b * P:(b + 1) * P], h_f[:, b, j * P:(j + 1) * P], ident[:])
                mm.then_inc(ht_mm, 1)

            def score_rows(g, j):
                wait(pe, ht_low, 2 * g + 2)
                if first(g):
                    pe.wait_ge(wa_ready, 2)
                wait_bank()
                for k in range(KF):
                    pe.matmul(bank_of("F")[:], wa_hl[:, k, :], blk_h[:, k, :], start=(k == 0), stop=False)
                    mm = pe.matmul(bank_of("F")[:], wa_h[:, k, :], blk_l[:, k, :], start=False, stop=(k == KF - 1))
                mm.then_inc(f_mm, 1)

            def scores(psum, f1_rows, f2_rows):
                pe.matmul(psum[:], ident_b[:], mask[:].rearrange("p a m -> p (a m)"), start=True, stop=False,
                          skip_group_check=True)
                pe.matmul(psum[:], f1_rows, pick_f1[:].rearrange("p a m -> p (a m)"), start=False, stop=False,
                          skip_group_check=True)
                for k in range(GB):
                    mm = pe.matmul(psum[:, k * P:(k + 1) * P], pick_f2[:, k, :], f2_rows[k], start=False,
                                   stop=(k == GB - 1), skip_group_check=True)
                return mm

            def score_tile(g, j):
                wait(pe, f_low, g + 1)
                if first(g, j):
                    pe.wait_ge(consts, 5)
                    pe.wait_ge(mask_ready, 1)
                wait_bank()
                mine = rows[:, j * P:(j + 1) * P]
                scores(bank_of("S", j), mine, [mine] * H).then_inc(s_mm, 1)

            def prob_turn(g, j):
                wait(pe, s_prob, GB * g + j + 1)
                wait_bank()
                for k in range(H):
                    mm = pe.transpose(bank_of("PT", j)[:, k * P:(k + 1) * P], z[:, j, k, :], ident[:])
                mm.then_inc(pt_mm, 1)

            def attend(g, j):
                b, k = divmod(j, KF)
                wait(pe, pt_low, GB * g + b + 1)
                wait(pe, h_low, g + 1)
                wait_bank()
                cols = slice(k * P, (k + 1) * P)
                three(bank_of("G", j)[:], [(h_h[:, b, cols], h_l[:, b, cols], pt_h[:, b % 2, :], pt_l[:, b % 2, :])]
                      ).then_inc(g_mm, 1)

            def project(g, j):
                head, ob = divmod(j, O1 // P)
                wait(pe, g_low, GB * KF * g + GB * KF)
                if first(g, j):
                    pe.wait_ge(wheads_low, 1)
                wait_bank()
                cols = slice(ob * P, (ob + 1) * P)
                three(bank_of("W", j)[:], [
                    (wh_h[:, head * KF + k, cols], wh_l[:, head * KF + k, cols],
                     g_h[:, k, head, :, :].rearrange("p b n -> p (b n)"), g_l[:, k, head, :, :].rearrange("p b n -> p (b n)"))
                    for k in range(KF)]).then_inc(w_mm, 1)

            def project2(g, j):
                wait_bank()
                if first(g, j):
                    pe.wait_ge(woa_ready, 1)
                    pe.wait_ge(late_low, 1)
                psum = bank_of("N", j)[:, 0:NAUG]
                cols = slice(j * P, (j + 1) * P)
                for k in range(KH):
                    if j == 0:
                        wait(pe, w_low, KH * g + k + 1)
                    pe.matmul(psum, h1_h[:, k, cols], wo_h[:, k, :], start=(k == 0), stop=False)
                    pe.matmul(psum, h1_h[:, k, cols], wo_l[:, k, :], start=False, stop=False)
                    mm = pe.matmul(psum, h1_l[:, k, cols], wo_h[:, k, :], start=False, stop=(k == KH - 1))
                mm.then_inc(n_mm, 1)

            def score_rows2(g, j):
                wait(pe, n_low, GB * g + GB)
                wait_bank()
                pe.transpose(bank_of("fT")[:, 0:P], f2n[:], ident[:]).then_inc(ft_mm, 1)

            def score_tile2(g, j):
                wait(pe, ft_low, g + 1)
                wait_bank()
                scores(bank_of("R"), rows2[:], [rows2[:]] * GB).then_inc(r_mm, 1)

            def prob_turn2(g, j):
                wait(pe, r_prob, g + 1)
                wait_bank()
                for b in range(GB):
                    mm = pe.transpose(bank_of("P2")[:, b * P:(b + 1) * P], z[:, GB, b, :], ident[:])
                mm.then_inc(p2_mm, 1)

            def attend2(g, j):
                wait(pe, p2_low, g + 1)
                wait_bank()
                for k in range(2):
                    b = 2 * j + k
                    mm = three(bank_of("O", j)[:, k * O2:(k + 1) * O2], [(p2_h[:, b, :], p2_l[:, b, :], wh2_h[:, b, :], wh2_l[:, b, :])])
                mm.then_inc(o_mm, 1)

            def turn_o(g, j):
                wait(pe, o_elu, 2 * g + 2)
                wait_bank()
                for b in range(GB):
                    mm = pe.transpose(bank_of("oT", j)[:, b * P:(b + 1) * P], o_f[b // 2][:, b % 2, j * P:(j + 1) * P], ident[:])
                mm.then_inc(ot_mm, 1)

            def mlp_in(g, j):
                wait(pe, ot_low, KO * g + KO)
                if first(g, j):
                    pe.wait_ge(late_low, 3)
                wait_bank()
                cols = slice(j * P, (j + 1) * P)
                three(bank_of("M", j)[:], [(w1_h[:, k, cols], w1_l[:, k, cols], o_h[:, k, :], o_l[:, k, :])
                                            for k in range(KO)]).then_inc(m_mm, 1)

            def mlp_out(g, j):
                wait(pe, m_low, KD * g + KD)
                wait_bank()
                for b in range(2):
                    n = slice((2 * j + b) * P, (2 * j + b + 1) * P)
                    mm = three(bank_of("Y", j)[:, b * O2:(b + 1) * O2],
                               [(blk_h[:, k, n], blk_l[:, k, n], w2_h[:, k, :], w2_l[:, k, :]) for k in range(KD)])
                mm.then_inc(y_mm, 1)

            def keep_warm(n, j):
                wait_bank()
                for _ in range(n):
                    pe.matmul(bank[j][:], pick_f1[:, 0, :], pick_f1[:].rearrange("p a m -> p (a m)"), start=True, stop=True)

            pe.wait_ge(patterns, 4)
            pe.wait_ge(consts, 4)
            run(pe, PE_START, PE_STEP, PE_END, {
                "hT": transposed, "F": score_rows, "S": score_tile, "PT": prob_turn, "G": attend, "W": project,
                "N": project2, "fT": score_rows2, "R": score_tile2, "P2": prob_turn2, "O": attend2, "oT": turn_o, "M": mlp_in,
                "Y": mlp_out, "warm": keep_warm}, bank_user)

        @block.scalar
        def _(act):
            def high(dst, src, ready, n, done):
                wait(act, ready, n)
                act.activation(dst, src, ACT.Copy).then_inc(done, 1)

            def ln_relu_op(g, j):
                wait(act, ln_bias, g + 1)
                wait(act, ht_mm, KF * g)
                wait(act, h_low, g)
                for b in range(GB):
                    act.activation(h_f[:, b, :], x_in[:, b, :], ACT.Relu, bias=nbias1[:, b:b + 1],
                                   scale=rstd1[:, b:b + 1]).then_inc(ln_relu, 1)

            def ht(g, j):
                wait(act, f_mm, g)
                wait(act, y_mm, 2 * (g - 2))
                high(blk_h[:, j, :], bank_of("hT", j)[:], ht_mm, KF * g + j + 1, ht_high)

            def f(g, j):
                wait(act, s_mm, GB * g)
                high(rows[:], bank_of("F")[:], f_mm, g + 1, f_high)

            def slope_of(psum, buf, ready, n, done):
                wait(act, ready, n)
                act.activation(buf[:].rearrange("p a m -> p (a m)"), psum[:], ACT.Copy, scale=LEAKY).then_inc(done, 1)

            def s(g, j):
                wait(act, s_leaky, GB * g + j - 1)
                slope_of(bank_of("S", j), slope[j % 2], s_mm, GB * g + j + 1, s_slope)

            def r(g, j):
                wait(act, r_leaky, g)
                if first(g):
                    act.wait_ge(woa_ready, 1)
                slope_of(bank_of("R"), slope[2], r_mm, g + 1, r_slope)

            def exps(tile, ready, n, done):
                wait(act, ready, n)
                act.activation(z[:, tile, :, :], z[:, tile, :, :], ACT.Exp).then_inc(done, 1)

            def pt(g, j):
                wait(act, g_mm, GB * KF * g + KF * (j - 1))
                high(pt_h[:, j % 2, :], bank_of("PT", j)[:], pt_mm, GB * g + j + 1, pt_high)

            def gg(g, j):
                wait(act, w_mm, KH * g)
                b, k = divmod(j, KF)
                high(g_h[:, k, :, b, :], bank_of("G", j)[:].rearrange("p (h n) -> p h n", h=H), g_mm,
                     GB * KF * g + j + 1, g_high)

            def w_first(g, j):
                wait(act, w_mm, KH * g + j + 1)
                wait(act, w_elu, KH * g + j - 1)
                act.activation(elu_exp[j % 2], bank_of("W", j)[:], ACT.Relu, scale=-1.0).then_inc(w_neg, 1)

            def w_second(g, j):
                wait(act, w_neg, KH * g + j + 1)
                act.activation(elu_exp[j % 2], elu_exp[j % 2], ACT.Exp, scale=-1.0).then_inc(w_exp, 1)

            def w_split(g, j):
                wait(act, n_mm, GB * g)
                high(h1_h[:, j, :], elu_out[j % 4], w_elu, KH * g + j + 1, w_high)

            def nn(g, j):
                wait(act, o_mm, 2 * g)
                high(wh2_h[:, j, :], bank_of("N", j)[:, 0:O2], n_mm, GB * g + j + 1, n_high)

            def ft(g, j):
                high(rows2[:], bank_of("fT")[:, 0:P], ft_mm, g + 1, ft_high)

            def p2(g, j):
                high(p2_h[:].rearrange("p b n -> p (b n)"), bank_of("P2")[:], p2_mm, g + 1, p2_high)

            def o_first(g, j):
                wait(act, o_mm, 2 * g + j + 1)
                wait(act, o_elu, 2 * g + j - 1)
                if first(g, j):
                    act.wait_ge(late_low, 3)
                act.activation(o_exp[j], bank_of("O", j)[:], ACT.Relu, scale=-1.0).then_inc(o_neg, 1)

            def o_second(g, j):
                wait(act, o_neg, 2 * g + j + 1)
                act.activation(o_exp[j], o_exp[j], ACT.Exp, scale=-1.0).then_inc(o_exp_done, 1)

            def turned_o(g, j):
                high(o_h[:, j, :], bank_of("oT", j)[:], ot_mm, KO * g + j + 1, ot_high)

            def m(g, j):
                wait(act, m_mm, KD * g + j + 1)
                wait(act, m_low, KD * g + j - 1)
                if first(g, j):
                    act.wait_ge(vec_loaded, 64)
                act.activation(m_f[j], bank_of("M", j)[:], ACT.Relu, bias=b1_col[:, j:j + 1]).then_inc(m_relu, 1)

            def m_split(g, j):
                wait(act, f_mm, min(g + 3, NG) if isinstance(g, int) else g + 3)
                high(blk_h[:, j, :], m_f[j], m_relu, KD * g + j + 1, m_high)

            def y_norm_op(g, j):
                for k, lo, hi in y_parts(g):
                    wait(act, y_nbias, g + 1 + k)
                    for b in range(lo, hi):
                        act.activation(y[:, b, :], y[:, b, :], ACT.Identity, bias=nbias2[:, b:b + 1],
                                       scale=rstd2[:, b:b + 1]).then_inc(y_norm, 1)

            def wheads_split(g, j):
                for loaded in wheads_loaded:
                    act.wait_ge(loaded, 16)
                act.activation(wh_h[:], wheads_f, ACT.Copy).then_inc(wheads_high, 1)

            def wout_split(g, j):
                act.wait_ge(wout_loaded, 16)
                act.activation(wo_h[:, :, 0:O2], wout_f, ACT.Copy).then_inc(late_high, 1)

            def ffn_split(g, j):
                act.wait_ge(ffn_loaded, 32)
                act.activation(w1_h[:], ffn_f[:, 0:2, :], ACT.Copy).then_inc(late_high, 1)
                act.activation(w2_h[:], ffn_f[:, 2:4, :], ACT.Copy).then_inc(late_high, 1)

            run(act, ACT_START, ACT_STEP, ACT_END, {
                "LNr": ln_relu_op, "hTh": ht, "Fh": f, "Su": s, "Ru": r, "PTh": pt, "Gh": gg, "Wn": w_first,
                "We": w_second, "Wh": w_split, "Nh": nn, "fTh": ft, "P2h": p2, "On": o_first, "Oe": o_second,
                "oTh": turned_o, "Mr": m, "Mh": m_split, "Yn": y_norm_op,
                "Se": lambda g, j: exps(j, s_shift, GB * g + j + 1, s_exp),
                "Re": lambda g, j: exps(GB, r_shift, g + 1, r_exp),
                "whH": wheads_split, "woH": wout_split, "wfH": ffn_split})

        @block.vector
        def _(dve):
            def low(dst, psum, high, ready, n, done):
                wait(dve, ready, n)
                dve.tensor_tensor(dst, psum, high.bitcast(F32), ALU.subtract).then_inc(done, 1)

            def stats(src, st, mean, diff, ve, graphs, stats_before, steps_before, s_stats, s_step, s_var):
                lo, hi = graphs
                for b in range(lo, hi):
                    dve.bn_stats(st[:, b, :], src[:, b, :]).then_inc(s_stats, 1)
                st, mean, diff, ve = st[:, lo:hi, :], mean[:, lo:hi], diff[:, lo:hi], ve[:, lo:hi]
                wait(dve, s_stats, stats_before + hi - lo)
                dve.tensor_tensor(diff, st[:, :, 1], st[:, :, 4], ALU.subtract).then_inc(s_step, 1)
                dve.scalar_tensor_tensor(ve, st[:, :, 2], F * LN_EPS, st[:, :, 5], ALU.add, ALU.add).then_inc(s_step, 1)
                dve.tensor_tensor(mean, st[:, :, 1], st[:, :, 4], ALU.add).then_inc(s_step, 1)
                wait(dve, s_step, steps_before + 1)
                dve.scalar_tensor_tensor(diff, diff, 0.25, diff, ALU.mult, ALU.mult).then_inc(s_step, 1)
                wait(dve, s_step, steps_before + 4)
                dve.scalar_tensor_tensor(ve, ve, 1.0 / F, diff, ALU.mult, ALU.add).then_inc(s_var, 1)

            def ln_stats_op(g, j):
                wait(dve, x_in_ready, 16 * g + 16)
                wait(dve, ln_rstd, g)
                stats(x_in, st1, mean1, diff1, ve1, (0, GB), GB * g, 4 * g, ln_stats, ln_step, ln_var)

            def ln_bias_op(g, j):
                wait(dve, ln_rstd, g + 1)
                wait(dve, ln_relu, GB * g)
                dve.scalar_tensor_tensor(nbias1[:], mean1[:], -0.5, rstd1[:], ALU.mult, ALU.mult).then_inc(ln_bias, 1)

            def ht(g, j):
                low(blk_l[:, j, :], bank_of("hT", j)[:], blk_h[:, j, :], ht_high, KF * g + j + 1, ht_low)

            def h_split(g, j):
                wait(dve, ln_relu, GB * g + GB)
                wait(dve, g_mm, GB * KF * g)
                wait(dve, h_low, g)
                dve.tensor_copy(h_h[:], h_f[:]).then_inc(h_high, 1)

            def f(g, j):
                lows = slice(PART, 2 * PART)
                low(rows[lows, :], bank_of("F")[lows, :], rows[lows, :], f_high, g + 1, f_low)

            def leaky(tile, psum, buf, ready, done, n):
                wait(dve, ready, n)
                dve.tensor_tensor(z[:, tile, :, :].rearrange("p a m -> p (a m)"), psum[:],
                                  buf[:].rearrange("p a m -> p (a m)"), ALU.max).then_inc(done, 1)

            def row_max(tile, ready, done, n):
                wait(dve, ready, n)
                dve.tensor_reduce(zmax[:, tile, :], z[:, tile, :, :], AX_X, ALU.max).then_inc(done, 1)

            def sums(tile, ready, s_s, s_i, n):
                wait(dve, ready, n)
                dve.tensor_reduce(zsum[:, tile, :], z[:, tile, :, :], AX_X, ALU.add).then_inc(s_s, 1)
                wait(dve, s_s, n)
                dve.reciprocal(zinv[:, tile, :], zsum[:, tile, :]).then_inc(s_i, 1)

            def s_leaky_op(g, j):
                wait(dve, pt_mm, GB * (g - 1) + j + 1)
                leaky(j, bank_of("S", j), slope[j % 2], s_slope, s_leaky, GB * g + j + 1)

            def r_leaky_op(g, j):
                wait(dve, p2_mm, g)
                leaky(GB, bank_of("R"), slope[2], r_slope, r_leaky, g + 1)

            def pt(g, j):
                low(pt_l[:, j % 2, :], bank_of("PT", j)[:], pt_h[:, j % 2, :], pt_high, GB * g + j + 1, pt_low)

            def gg(g, j):
                b, k = divmod(j, KF)
                low(g_l[:, k, :, b, :], bank_of("G", j)[:].rearrange("p (h n) -> p h n", h=H), g_h[:, k, :, b, :],
                    g_high, GB * KF * g + j + 1, g_low)

            def w(g, j):
                wait(dve, w_exp, KH * g + j + 1)
                wait(dve, w_low, KH * g + j - 3)
                dve.scalar_tensor_tensor(elu_out[j % 4], elu_exp[j % 2], -1.0, bank_of("W", j)[:], ALU.add, ALU.max
                                         ).then_inc(w_elu, 1)

            def nn(g, j):
                psum = bank_of("N", j)
                wait(dve, ft_mm, g)
                low(wh2_l[:, j, :], psum[:, 0:O2], wh2_h[:, j, :], n_high, GB * g + j + 1, n_part)
                cols = f2n[:, 0:2 * PART].rearrange("p (r c) -> p r c", r=2)[:, :, j:j + GB + 1:GB]
                dve.tensor_copy(cols, psum[:, O2:NAUG].unsqueeze(1).to_broadcast([P, 2, 2])).then_inc(n_low, 1)

            def ft(g, j):
                lows = slice(PART, 2 * PART)
                low(rows2[lows, :], bank_of("fT")[lows, 0:P], rows2[lows, :], ft_high, g + 1, ft_low)

            def p2(g, j):
                low(p2_l[:].rearrange("p b n -> p (b n)"), bank_of("P2")[:], p2_h[:].rearrange("p b n -> p (b n)"),
                    p2_high, g + 1, p2_low)

            def o(g, j):
                wait(dve, o_exp_done, 2 * g + j + 1)
                wait(dve, ot_mm, KO * g)
                wait(dve, o_bias, 2 * g)
                dve.scalar_tensor_tensor(o_f[j].rearrange("p b c -> p (b c)"), o_exp[j], -1.0, bank_of("O", j)[:],
                                         ALU.add, ALU.max).then_inc(o_elu, 1)

            def turned_o(g, j):
                low(o_l[:, j, :], bank_of("oT", j)[:], o_h[:, j, :], ot_high, KO * g + j + 1, ot_low)

            def m(g, j):
                low(blk_l[:, j, :], m_f[j], blk_h[:, j, :], m_high, KD * g + j + 1, m_low)

            def yy(g, j):
                wait(dve, y_mm, 2 * g + j + 1)
                wait(dve, o_bias, 2 * g + j + 1)
                pair = y[:, 2 * j:2 * j + 2, :].rearrange("p b c -> p (b c)")
                dve.tensor_tensor(pair, bank_of("Y", j)[:], pair, ALU.add).then_inc(y_sum, 1)

            def y_stats_op(g, j):
                for k, lo, hi in y_parts(g):
                    wait(dve, y_sum, 2 * g + hi // 2)
                    stats(y, st2, mean2, diff2, ve2, (lo, hi), GB * g + lo, 4 * g + 4 * k, y_stats, y_step, y_var)

            def y_nbias_op(g, j):
                for k, lo, hi in y_parts(g):
                    wait(dve, y_rstd, g + 1 + k)
                    dve.scalar_tensor_tensor(nbias2[:, lo:hi], mean2[:, lo:hi], -0.5, rstd2[:, lo:hi], ALU.mult, ALU.mult
                                             ).then_inc(y_nbias, 1)

            def y_last(g, j):
                wait(dve, xb_ready, g + 1)
                res = residual_of(g)
                for k, lo, hi in y_parts(g):
                    wait(dve, y_gamma, g + 1 + k)
                    dve.tensor_tensor(y[:, lo:hi, :], y[:, lo:hi, :], res[:, lo:hi, :], ALU.add).then_inc(y_done, 1)

            dve.wait_ge(patterns, 4)
            dve.tensor_copy(ident_b[:], ident[:]).then_inc(consts, 1)
            dve.tensor_reduce(picks[:], ident[:, 0:2 * PART].rearrange("p (a r) -> p a r", a=2)[:, :, 0:4 * H]
                              .rearrange("p a (l c) -> p c a l", l=2), AX_XY, ALU.add).then_inc(consts, 1)
            dve.wait_ge(consts, 2)
            for k, pick in enumerate((pick_f1, pick_f2)):
                dve.tensor_copy(pick[:], picks[:, k * H:(k + 1) * H].unsqueeze(2).to_broadcast([P, H, P])).then_inc(consts, 1)
            dve.memset(wa_f[:], 0.0).then_inc(wa_steps, 1)
            done = 1 + 2 * H * KF

            def wheads_a(g, h):
                if h % 2 == 0:
                    dve.wait_ge(wheads_loaded[h // 2], 16)
                    dve.wait_ge(avec_loaded[h // 2], 16)
                for k in range(KF):
                    for half in range(2):
                        a = avec_f[h // 2][:, 2 * (h % 2) + half, :]
                        dve.wait_ge(wa_steps, max(1, 2 * (h * KF + k) + half))
                        dve.tensor_tensor_reduce(junk[half], wheads_f[:, h * KF + k, :], a, 1.0, 0.0, ALU.mult, ALU.add,
                                                 wa_f[:, k, h + H * half:h + H * half + 1]).then_inc(wa_steps, 1)

            def wheads_a_split(g, j):
                dve.wait_ge(wa_steps, done)
                dve.tensor_copy(wa_f[:, :, PART:PART + 2 * H], wa_f[:, :, 0:2 * H]).then_inc(wa_steps, 1)
                dve.wait_ge(wa_steps, done + 1)
                dve.tensor_copy(wa_h[:], wa_f[:]).then_inc(wa_steps, 1)
                dve.wait_ge(wa_steps, done + 2)
                dve.tensor_copy(wa_hl[:], wa_h[:]).then_inc(wa_steps, 1)
                dve.wait_ge(wa_steps, done + 3)
                for start in (0, PART):
                    part = slice(start, start + 2 * H)
                    dve.tensor_tensor(wa_hl[:, :, start + 2 * H:start + 4 * H], wa_f[:, :, part], wa_h[:, :, part].bitcast(F32),
                                      ALU.subtract).then_inc(wa_ready, 1)

            def mask_from_adj(g, j):
                dve.wait_ge(adj_loaded, 16)
                dve.tensor_scalar(z[:, GB, 1, :], z[:, GB, 0, :].bitcast(I32), 0, 1.0, ALU.is_gt, ALU.subtract).then_inc(consts, 1)
                dve.wait_ge(consts, 5)
                dve.tensor_scalar(mask[:], z[:, GB, 1, :].unsqueeze(1).to_broadcast([P, GB, P]), MASKED, None, ALU.mult
                                  ).then_inc(mask_ready, 1)

            def wout_a(g, j):
                if j == 0:
                    dve.wait_ge(wout_loaded, 16)
                    dve.wait_ge(aout_loaded, 16)
                for k in (2 * j, 2 * j + 1):
                    for half in range(2):
                        dve.wait_ge(wa_steps, done + 2 + 2 * k + half)
                        dve.tensor_tensor_reduce(junk2[half], wout_f[:, k, :], aout_f[:, half * O2:(half + 1) * O2],
                                                 1.0, 0.0, ALU.mult, ALU.add, wo_a[:, k, half:half + 1]).then_inc(wa_steps, 1)

            def wout_a_split(g, j):
                dve.wait_ge(wa_steps, done + 3 + 2 * KH)
                dve.tensor_copy(wo_h[:, :, O2:NAUG], wo_a[:]).then_inc(wa_steps, 1)
                dve.wait_ge(wa_steps, done + 4 + 2 * KH)
                dve.tensor_tensor(wo_l[:, :, O2:NAUG], wo_a[:], wo_h[:, :, O2:NAUG].bitcast(F32), ALU.subtract).then_inc(woa_ready, 1)

            run(dve, DVE_START, DVE_STEP, DVE_END, {
                "LNs": ln_stats_op, "LNb": ln_bias_op, "hTl": ht, "Hh": h_split, "Fl": f, "PTl": pt, "Gl": gg, "Wv": w,
                "Nl": nn, "fTl": ft, "P2l": p2, "Ov": o, "oTl": turned_o, "Ml": m, "Yb": yy, "Yst": y_stats_op, "Ynb": y_nbias_op,
                "Yo": y_last, "Sl": s_leaky_op, "Rl": r_leaky_op,
                "Sm": lambda g, j: row_max(j, s_leaky, s_max, GB * g + j + 1),
                "Rm": lambda g, j: row_max(GB, r_leaky, r_max, g + 1),
                "Sr": lambda g, j: sums(j, s_exp, s_sum, s_inv, GB * g + j + 1),
                "Rr": lambda g, j: sums(GB, r_exp, r_sum, r_inv, g + 1),
                "WA": wheads_a, "WAf": wheads_a_split, "MK": mask_from_adj, "OA": wout_a, "OAf": wout_a_split})

        @block.gpsimd
        def _(pool):
            def low(dst, value, high, ready, n, done):
                wait(pool, ready, n)
                pool.tensor_tensor(dst, value, high.bitcast(F32), ALU.subtract).then_inc(done, 1)

            def inverse_root(dst, var, ready, n, done):
                wait(pool, ready, n)
                pool.tensor_tensor(dst, var, half_power[:, 0:dst.shape[1]], ALU.pow).then_inc(done, 1)

            def ln_root(g, j):
                wait(pool, ln_relu, GB * g)
                inverse_root(rstd1[:], ve1[:], ln_var, g + 1, ln_rstd)

            def y_root(g, j):
                wait(pool, y_norm, GB * g)
                for k, lo, hi in y_parts(g):
                    inverse_root(rstd2[:, lo:hi], ve2[:, lo:hi], y_var, g + 1 + k, y_rstd)

            def h_split(g, j):
                low(h_l[:], h_f[:], h_h[:], h_high, g + 1, h_low)

            def by_block(tile, op, factors, ready, n, done):
                wait(pool, ready, n)
                pool.tensor_tensor(z[:, tile, :, :], z[:, tile, :, :],
                                   factors[:, tile, :].unsqueeze(2).to_broadcast([P, GB, P]), op).then_inc(done, 1)

            def w(g, j):
                low(h1_l[:, j, :], elu_out[j % 4], h1_h[:, j, :], w_high, KH * g + j + 1, w_low)

            def o_plus_b2(g, j):
                wait(pool, o_elu, 2 * g + j + 1)
                wait(pool, out_stored, 16 * g)
                if first(g, j):
                    pool.wait_ge(vec_loaded, 64)
                    pool.wait_ge(woa_ready, 1)
                pool.tensor_tensor(y[:, 2 * j:2 * j + 2, :], o_f[j], b2_bc[:].unsqueeze(1).to_broadcast([P, 2, O2]), ALU.add
                                   ).then_inc(o_bias, 1)

            def residual(g, j):
                res = residual_of(g)
                if res is x_in:
                    wait(pool, ln_relu, GB * NG)
                else:
                    wait(pool, x_res_ready, 16 * g + 16)
                if first(g):
                    pool.wait_ge(vec_loaded, 64)
                pool.tensor_tensor(res[:], res[:], beta_bc[:].unsqueeze(1).to_broadcast([P, GB, O2]), ALU.add
                                   ).then_inc(xb_ready, 1)

            def y_scale(g, j):
                for k, lo, hi in y_parts(g):
                    wait(pool, y_norm, GB * g + hi)
                    pool.tensor_tensor(y[:, lo:hi, :], y[:, lo:hi, :],
                                       gamma_bc[:].unsqueeze(1).to_broadcast([P, hi - lo, O2]), ALU.mult).then_inc(y_gamma, 1)

            pool.memset(half_power[:], -0.5).then_inc(patterns, 1)
            pool.memset(f2n[:], 0.0).then_inc(patterns, 1)
            pool.memset(ident[:], 0.0).then_inc(patterns, 1)
            pool.wait_ge(patterns, 3)
            pool.affine_select(out=ident[:], in_=ident[:], compare_op=ALU.not_equal, fill=1.0, base=0,
                               pattern=[[-1, P]], channel_multiplier=1).then_inc(patterns, 1)

            def wheads_split(g, j):
                pool.wait_ge(wheads_high, 1)
                pool.tensor_tensor(wh_l[:], wheads_f, wh_h[:].bitcast(F32), ALU.subtract).then_inc(wheads_low, 1)

            def wout_split(g, j):
                pool.wait_ge(late_high, 1)
                pool.tensor_tensor(wo_l[:, :, 0:O2], wout_f, wo_h[:, :, 0:O2].bitcast(F32), ALU.subtract).then_inc(late_low, 1)

            def ffn_split(g, j):
                for k, (dst, high) in enumerate(((w1_l, w1_h), (w2_l, w2_h))):
                    pool.wait_ge(late_high, k + 2)
                    pool.tensor_tensor(dst[:], ffn_f[:, 2 * k:2 * k + 2, :], high[:].bitcast(F32), ALU.subtract).then_inc(late_low, 1)

            run(pool, POOL_START, POOL_STEP, POOL_END, {
                "LNp": ln_root, "Hl": h_split, "Wl": w, "ob": o_plus_b2, "xb": residual, "Yp": y_root, "Yg": y_scale,
                "Ss": lambda g, j: by_block(j, ALU.subtract, zmax, s_max, GB * g + j + 1, s_shift),
                "Sp": lambda g, j: by_block(j, ALU.mult, zinv, s_inv, GB * g + j + 1, s_prob),
                "Rs": lambda g, j: by_block(GB, ALU.subtract, zmax, r_max, g + 1, r_shift),
                "Rp": lambda g, j: by_block(GB, ALU.mult, zinv, r_inv, g + 1, r_prob),
                "whL": wheads_split, "woL": wout_split, "wfL": ffn_split})


_INS = ["x", "adj", "L0_gnn_W_heads", "L0_gnn_a_heads", "L0_gnn_W_out", "L0_gnn_a_out", "L0_gnn_w1", "L0_gnn_b1",
        "L0_gnn_w2", "L0_gnn_b2", "L0_gnn_ln_gamma", "L0_gnn_ln_beta"]


def kernel(**inputs):
    import concourse.bacc as _bacc
    from concourse.bass_utils import run_bass_kernel_spmd as _run

    nc = _bacc.Bacc("TRN2", target_bir_lowering=False, num_devices=1, dynamic_dma_scratch_size=1024)
    arrays, args = {}, []
    for name in _INS:
        a = np.ascontiguousarray(inputs[name])
        arrays[f"in_{name}_dram"] = a
        args.append(nc.dram_tensor(f"in_{name}_dram", a.shape, mybir.dt.from_np(a.dtype), kind="ExternalInput").ap())
    shape = inputs["x"].shape
    out = nc.dram_tensor("out_dram", shape, F32, kind="ExternalOutput").ap()
    gat_kernel(nc, *args, out)
    r = _run(nc, [arrays], core_ids=[0])
    return r.results[0]["out_dram"]
```
